# Optimizing a Trainium2 kernel written in Bass

```python
import numpy as np
import jax
import jax.numpy as jnp

def _softmax(x, axis=-1):
    return jax.nn.softmax(x, axis=axis)

def _gelu(x):
    return jax.nn.gelu(x, approximate=True)

def _silu(x):
    return jax.nn.silu(x)

def _sigmoid(x):
    return jax.nn.sigmoid(x)

def _layernorm(x, axis=-1, eps=1e-05):
    m = jnp.mean(x, axis=axis, keepdims=True)
    v = jnp.var(x, axis=axis, keepdims=True)
    return (x - m) / jnp.sqrt(v + eps)

def _scatter_add(tgt, idx, src, axis=0):
    return tgt.at[idx].add(src)

def _segment_sum(src, seg, n):
    return jax.ops.segment_sum(src, seg, n)
kernel_name = 'mk_recurrent_d4_jaxref_r8_670203'

def setup_inputs(seed: int=0):
    np.random.seed(seed)
    _w = jnp.asarray

    def _L0_attn_setup():
        import jax, jax.numpy as jnp
        import numpy as np
        B, S, D, H = (2, 256, 128, 16)
        DH = D // H
        LAMBDA_INIT = 0.8
        EPS = 1e-05

        def _forward(inputs, wq0, wq1, wk0, wk1, wv, wo, l0, l1, l2, l3, ln_w, ln_b):
            b, s, d = inputs.shape

            def proj(w):
                return jnp.einsum('bsd,de->bse', inputs, w).reshape(b, s, H, DH).transpose(0, 2, 1, 3)
            q0, q1 = (proj(wq0), proj(wq1))
            k0, k1 = (proj(wk0), proj(wk1))
            v = proj(wv)
            scale = jax.lax.rsqrt(jnp.float32(DH))
            slopes = 2.0 ** (-8.0 * jnp.arange(1, H + 1, dtype=jnp.float32) / H)
            pos = jnp.arange(s, dtype=jnp.float32)
            pos_diff = pos[:, None] - pos[None, :]
            bias = slopes[None, :, None, None] * pos_diff[None, None, :, :]
            causal = jnp.where(jnp.triu(jnp.ones((s, s), bool), 1), -jnp.inf, 0.0)[None, None]
            s0 = jnp.einsum('bhqd,bhkd->bhqk', q0, k0) * scale - bias + causal
            s1 = jnp.einsum('bhqd,bhkd->bhqk', q1, k1) * scale - bias + causal
            w0 = jax.nn.softmax(s0, axis=-1)
            w1 = jax.nn.softmax(s1, axis=-1)
            lamb = -jnp.exp(jnp.dot(l0, l1)) + LAMBDA_INIT + (-jnp.exp(jnp.dot(l2, l3)) + LAMBDA_INIT)
            diff_weights = w0 - lamb * w1
            heads = jnp.einsum('bhqk,bhkd->bhqd', diff_weights, v).transpose(0, 2, 1, 3)
            mu = jnp.mean(heads, axis=-1, keepdims=True)
            var = jnp.mean((heads - mu) ** 2, axis=-1, keepdims=True)
            normed = (heads - mu) * jax.lax.rsqrt(var + EPS) * ln_w[None, None] + ln_b[None, None]
            attention = normed.reshape(b, s, H * DH)
            return jnp.einsum('bse,ed->bsd', attention, wo)
        key = jax.random.key(seed)
        ks = jax.random.split(key, 12)
        inp = {'inputs': jax.random.normal(ks[0], (B, S, D), jnp.float32), 'wq0': jax.random.normal(ks[1], (D, H * DH), jnp.float32) * 0.02, 'wq1': jax.random.normal(ks[2], (D, H * DH), jnp.float32) * 0.02, 'wk0': jax.random.normal(ks[3], (D, H * DH), jnp.float32) * 0.02, 'wk1': jax.random.normal(ks[4], (D, H * DH), jnp.float32) * 0.02, 'wv': jax.random.normal(ks[5], (D, H * DH), jnp.float32) * 0.02, 'wo': jax.random.normal(ks[6], (H * DH, D), jnp.float32) * 0.02, 'l0': jax.random.normal(ks[7], (DH,), jnp.float32) * 0.1, 'l1': jax.random.normal(ks[8], (DH,), jnp.float32) * 0.1, 'l2': jax.random.normal(ks[9], (DH,), jnp.float32) * 0.1, 'l3': jax.random.normal(ks[10], (DH,), jnp.float32) * 0.1, 'ln_w': jnp.ones((H, DH), jnp.float32), 'ln_b': jnp.zeros((H, DH), jnp.float32)}
        return inp
    _L0_attn_in = _L0_attn_setup()

    def _L0_ffn_setup():
        import jax, jax.numpy as jnp
        import numpy as np
        B, S, D, F, O = (4, 256, 128, 512, 128)
        E, NS, K = (4, 2, 2)
        key = jax.random.key(seed)
        ks = jax.random.split(key, 6)

        def w(k, shape, fan_in):
            return jax.random.normal(k, shape, jnp.float32) * fan_in ** (-0.5)
        return {'x': jax.random.normal(ks[0], (B, S, D), jnp.float32), 'gate_w': w(ks[1], (D, E), D), 'gate_b': jnp.zeros((E,), jnp.float32), 'sw1': w(ks[2], (NS, D, F), D), 'sb1': jnp.zeros((NS, F), jnp.float32), 'sw2': w(ks[3], (NS, F, O), F), 'sb2': jnp.zeros((NS, O), jnp.float32), 'rw1': w(ks[4], (E, D, F), D), 'rb1': jnp.zeros((E, F), jnp.float32), 'rw2': w(ks[5], (E, F, O), F), 'rb2': jnp.zeros((E, O), jnp.float32)}
    _L0_ffn_in = _L0_ffn_setup()

    def _L1_attn_setup():
        import jax, jax.numpy as jnp
        import numpy as np
        B, L, D = (2, 256, 128)
        H = 16
        DH = D // H
        FACTOR = 0.6
        U = max(1, min(L, int(FACTOR * L)))

        def _split_heads(x):
            b, l, d = x.shape
            return x.reshape(b, l, H, DH).transpose(0, 2, 1, 3)
        key = jax.random.key(seed)
        ks = jax.random.split(key, 9)
        s = 0.02
        return {'x': jax.random.normal(ks[0], (B, L, D), dtype=jnp.float32), 'Wq': jax.random.normal(ks[1], (D, D), dtype=jnp.float32) * s, 'bq': jnp.zeros((D,), dtype=jnp.float32), 'Wk': jax.random.normal(ks[2], (D, D), dtype=jnp.float32) * s, 'bk': jnp.zeros((D,), dtype=jnp.float32), 'Wv': jax.random.normal(ks[3], (D, D), dtype=jnp.float32) * s, 'bv': jnp.zeros((D,), dtype=jnp.float32), 'Wo': jax.random.normal(ks[4], (D, D), dtype=jnp.float32) * s, 'bo': jnp.zeros((D,), dtype=jnp.float32)}
    _L1_attn_in = _L1_attn_setup()

    def _L1_ffn_setup():
        import jax, jax.numpy as jnp
        import numpy as np
        H = 128
        E = 64
        K = 8
        G = 8
        TOPK_GROUP = 4
        I_MOE = 64
        I_SHARED = 256
        SCALE = 2.5

        def relu2(x):
            return jnp.square(jax.nn.relu(x))

        def _route(xf, router_w, correction_bias):
            T = xf.shape[0]
            logits = xf @ router_w.T
            scores = jax.nn.sigmoid(logits)
            sfc = scores + correction_bias[None, :]
            grp = sfc.reshape(T, G, E // G)
            top2, _ = jax.lax.top_k(grp, 2)
            group_scores = top2.sum(-1)
            _, gidx = jax.lax.top_k(group_scores, TOPK_GROUP)
            gmask = jnp.zeros((T, G), sfc.dtype).at[jnp.arange(T)[:, None], gidx].set(1.0)
            emask = jnp.repeat(gmask, E // G, axis=1)
            masked = jnp.where(emask > 0, sfc, 0.0)
            _, tidx = jax.lax.top_k(masked, K)
            tw = jnp.take_along_axis(scores, tidx, axis=1)
            tw = tw / (tw.sum(-1, keepdims=True) + 1e-20)
            return (tidx, tw * SCALE)
        key = jax.random.key(seed)
        ks = jax.random.split(key, 7)
        x = jax.random.normal(ks[0], (2, 128, H), dtype=jnp.float32)
        router_w = jax.random.normal(ks[1], (E, H), dtype=jnp.float32) * 0.02
        correction_bias = jax.random.normal(ks[2], (E,), dtype=jnp.float32) * 0.01
        up_w = jax.random.normal(ks[3], (E, H, I_MOE), dtype=jnp.float32) * 0.02
        down_w = jax.random.normal(ks[4], (E, I_MOE, H), dtype=jnp.float32) * 0.02
        shared_up_w = jax.random.normal(ks[5], (H, I_SHARED), dtype=jnp.float32) * 0.02
        shared_down_w = jax.random.normal(ks[6], (I_SHARED, H), dtype=jnp.float32) * 0.02
        return {'x': x, 'router_w': router_w, 'correction_bias': correction_bias, 'up_w': up_w, 'down_w': down_w, 'shared_up_w': shared_up_w, 'shared_down_w': shared_down_w}
    _L1_ffn_in = _L1_ffn_setup()

    def _L2_attn_setup():
        import jax, jax.numpy as jnp
        import numpy as np
        D = 128
        H = 4
        DK = D
        DV = 2 * D
        HK = DK // H
        HV = DV // H
        KCONV = 4
        EPS = 1e-05
        CHUNK = 64

        def causal_conv_silu(x, w):
            B, T, C = x.shape
            K = w.shape[1]
            xp = jnp.pad(x, ((0, 0), (K - 1, 0), (0, 0)))
            y = sum((xp[:, i:i + T, :] * w[:, i] for i in range(K)))
            return jax.nn.silu(y)

        def l2norm(x):
            return x * jax.lax.rsqrt(jnp.sum(x * x, -1, keepdims=True) + 1e-06)

        def _step(S, inp):
            q_t, k_t, v_t, g_t, b_t = inp
            S = S * jnp.exp(g_t)[..., None, None]
            v_eff = (v_t - jnp.einsum('bhk,bhkv->bhv', k_t, S)) * b_t[..., None]
            S = S + k_t[..., None] * v_eff[..., None, :]
            o_t = jnp.einsum('bhk,bhkv->bhv', q_t, S)
            return (S, o_t)

        @jax.checkpoint
        def _chunk(S, ch):
            return jax.lax.scan(_step, S, ch)

        def _forward(x, ln_w, ln_b, Wq, Wk, Wv, conv_q, conv_k, conv_v, Wb, Wa, A_log, dt_bias, Wg, norm_w, Wo):
            B, T, _ = x.shape
            mu = jnp.mean(x, -1, keepdims=True)
            var = jnp.mean((x - mu) ** 2, -1, keepdims=True)
            normed = (x - mu) * jax.lax.rsqrt(var + EPS) * ln_w + ln_b
            q = causal_conv_silu(normed @ Wq, conv_q)
            k = causal_conv_silu(normed @ Wk, conv_k)
            v = causal_conv_silu(normed @ Wv, conv_v)
            beta = jax.nn.sigmoid(normed @ Wb)
            g = -jnp.exp(A_log) * jax.nn.softplus(normed @ Wa + dt_bias)
            q = l2norm(q.reshape(B, T, H, HK)) * HK ** (-0.5)
            k = l2norm(k.reshape(B, T, H, HK))
            v = v.reshape(B, T, H, HV)
            nc = T // CHUNK

            def to_chunks(a):
                return jnp.moveaxis(a, 1, 0).reshape((nc, CHUNK, B) + a.shape[2:])
            qc, kc, vc, gc, bc = map(to_chunks, (q, k, v, g, beta))
            S0 = jnp.zeros((B, H, HK, HV), x.dtype)
            _, o = jax.lax.scan(_chunk, S0, (qc, kc, vc, gc, bc))
            o = jnp.moveaxis(o.reshape(T, B, H, HV), 0, 1)
            g_out = (normed @ Wg).reshape(B, T, H, HV)
            o = o * jax.lax.rsqrt(jnp.mean(o * o, -1, keepdims=True) + EPS) * norm_w
            o = o * g_out * jax.nn.sigmoid(g_out)
            return x + o.reshape(B, T, DV) @ Wo
        key = jax.random.key(seed)
        ks = jax.random.split(key, 16)
        B, T = (4, 256)
        p = lambda k, shape, s=0.02: jax.random.normal(k, shape, jnp.float32) * s
        return {'x': jax.random.normal(ks[0], (B, T, D), jnp.float32), 'ln_w': jnp.ones((D,), jnp.float32), 'ln_b': jnp.zeros((D,), jnp.float32), 'Wq': p(ks[1], (D, DK)), 'Wk': p(ks[2], (D, DK)), 'Wv': p(ks[3], (D, DV)), 'conv_q': p(ks[4], (DK, KCONV), 0.1), 'conv_k': p(ks[5], (DK, KCONV), 0.1), 'conv_v': p(ks[6], (DV, KCONV), 0.1), 'Wb': p(ks[7], (D, H)), 'Wa': p(ks[8], (D, H)), 'A_log': jnp.log(jax.random.uniform(ks[9], (H,), jnp.float32, 1.0, 16.0)), 'dt_bias': jnp.log(jnp.expm1(jax.random.uniform(ks[10], (H,), jnp.float32, 0.001, 0.1))), 'Wg': p(ks[11], (D, DV)), 'norm_w': jnp.ones((HV,), jnp.float32), 'Wo': p(ks[12], (DV, D))}
    _L2_attn_in = _L2_attn_setup()

    def _L2_ffn_setup():
        import jax, jax.numpy as jnp
        import numpy as np
        D_MODEL = 128
        FF = 512
        E = 8
        TOP_K = 2
        CAP_FACTOR = 1.25
        B, T = (4, 256)

        def _moe_forward(x, gate_w, gate_b, w1, b1, w2, b2):
            Bb, Tt, d = x.shape
            S = Bb * Tt
            C = int(CAP_FACTOR * S / E)
            xf = x.reshape(S, d)
            logits = xf @ gate_w + gate_b
            probs = jax.nn.softmax(logits, axis=1)
            topk_p, topk_i = jax.lax.top_k(probs, TOP_K)
            topk_pn = topk_p / jnp.sum(topk_p, axis=1, keepdims=True)
            rows = jnp.arange(S)
            w_te = jnp.zeros((S, E), xf.dtype).at[rows[:, None], topk_i].set(topk_pn)
            mask = jnp.zeros((S, E), bool).at[rows[:, None], topk_i].set(True)
            rank = jnp.cumsum(mask.astype(jnp.int32), axis=0)
            slot = jnp.where(mask & (rank <= C), rank - 1, C)
            e_grid = jnp.broadcast_to(jnp.arange(E), (S, E))
            t_grid = jnp.broadcast_to(rows[:, None], (S, E))
            buf = jnp.full((E, C + 1), S, jnp.int32).at[e_grid, slot].set(t_grid)
            idx = buf[:, :C]
            valid = idx < S
            x_pad = jnp.concatenate([xf, jnp.zeros((1, d), xf.dtype)], axis=0)
            xin = x_pad[idx]
            h = jax.nn.relu(jnp.einsum('ecd,edh->ech', xin, w1) + b1[:, None, :])
            out = jnp.einsum('ech,ehd->ecd', h, w2) + b2[:, None, :]
            w_pad = jnp.concatenate([w_te, jnp.zeros((1, E), xf.dtype)], axis=0)
            tok_w = w_pad[idx, jnp.arange(E)[:, None]]
            out = out * jnp.where(valid, tok_w, 0.0)[:, :, None]
            final = jnp.zeros((S + 1, d), xf.dtype).at[idx.reshape(-1)].add(out.reshape(-1, d))[:S]
            return final.reshape(Bb, Tt, d)
        key = jax.random.key(seed)
        ks = jax.random.split(key, 7)
        s = 0.02
        return {'x': jax.random.normal(ks[0], (B, T, D_MODEL), jnp.float32), 'gate_w': jax.random.normal(ks[1], (D_MODEL, E), jnp.float32) * s, 'gate_b': jnp.zeros((E,), jnp.float32), 'w1': jax.random.normal(ks[2], (E, D_MODEL, FF), jnp.float32) * s, 'b1': jnp.zeros((E, FF), jnp.float32), 'w2': jax.random.normal(ks[3], (E, FF, D_MODEL), jnp.float32) * s, 'b2': jnp.zeros((E, D_MODEL), jnp.float32)}
    _L2_ffn_in = _L2_ffn_setup()

    def _L3_attn_setup():
        import jax, jax.numpy as jnp
        import numpy as np
        N_HEADS = 16
        D_MODEL = 128
        D_HEAD = 64
        MAX_SEQ_LEN = 128

        def _pos_bias(rel_pos_bias, T):
            i = jnp.arange(T)[:, None]
            j = jnp.arange(T)[None, :]
            idx = jnp.clip(MAX_SEQ_LEN - 1 - (i - j), 0, MAX_SEQ_LEN - 1)
            bias = rel_pos_bias[:, idx]
            return jnp.where((j <= i)[None], bias, 0.0)
        key = jax.random.key(seed)
        ks = jax.random.split(key, 7)
        std = np.sqrt(2.0 / (D_MODEL + D_HEAD)).astype(np.float32)
        hd = N_HEADS * D_HEAD
        Wq = jax.random.normal(ks[0], (D_MODEL, hd), jnp.float32) * std
        Wk = jax.random.normal(ks[1], (D_MODEL, hd), jnp.float32) * std
        Wv = jax.random.normal(ks[2], (D_MODEL, hd), jnp.float32) * std
        Wo = jax.random.normal(ks[3], (hd, D_MODEL), jnp.float32) * (1.0 / np.sqrt(hd))
        bo = jnp.zeros((D_MODEL,), jnp.float32)
        rel_pos_bias = jax.random.normal(ks[4], (N_HEADS, MAX_SEQ_LEN), jnp.float32) * 0.02
        x = jax.random.normal(ks[5], (4, 128, D_MODEL), jnp.float32)
        return {'x': x, 'Wq': Wq, 'Wk': Wk, 'Wv': Wv, 'Wo': Wo, 'bo': bo, 'rel_pos_bias': rel_pos_bias}
    _L3_attn_in = _L3_attn_setup()

    def _L3_ffn_setup():
        import jax, jax.numpy as jnp
        import numpy as np
        DIM = 128
        HIDDEN = 384
        SCALE = 1.0 / 127.0

        def _dequant(w_int, dtype):
            return w_int.astype(dtype) * jnp.asarray(SCALE, dtype)
        key = jax.random.key(seed)
        k_x, k_g, k_u, k_d = jax.random.split(key, 4)
        x = jax.random.normal(k_x, (4, 256, DIM), dtype=jnp.float32)
        w_gate = jax.random.randint(k_g, (HIDDEN, DIM), -127, 128, dtype=jnp.int32)
        w_up = jax.random.randint(k_u, (HIDDEN, DIM), -127, 128, dtype=jnp.int32)
        w_down = jax.random.randint(k_d, (DIM, HIDDEN), -127, 128, dtype=jnp.int32)
        return {'x': x, 'w_gate': w_gate, 'w_up': w_up, 'w_down': w_down}
    _L3_ffn_in = _L3_ffn_setup()
    _d = {'L0_attn_inputs': _L0_attn_in['inputs'], 'L0_attn_wq0': _L0_attn_in['wq0'], 'L0_attn_wq1': _L0_attn_in['wq1'], 'L0_attn_wk0': _L0_attn_in['wk0'], 'L0_attn_wk1': _L0_attn_in['wk1'], 'L0_attn_wv': _L0_attn_in['wv'], 'L0_attn_wo': _L0_attn_in['wo'], 'L0_attn_l0': _L0_attn_in['l0'], 'L0_attn_l1': _L0_attn_in['l1'], 'L0_attn_l2': _L0_attn_in['l2'], 'L0_attn_l3': _L0_attn_in['l3'], 'L0_attn_ln_w': _L0_attn_in['ln_w'], 'L0_attn_ln_b': _L0_attn_in['ln_b'], 'L0_ffn_gate_w': _L0_ffn_in['gate_w'], 'L0_ffn_gate_b': _L0_ffn_in['gate_b'], 'L0_ffn_sw1': _L0_ffn_in['sw1'], 'L0_ffn_sb1': _L0_ffn_in['sb1'], 'L0_ffn_sw2': _L0_ffn_in['sw2'], 'L0_ffn_sb2': _L0_ffn_in['sb2'], 'L0_ffn_rw1': _L0_ffn_in['rw1'], 'L0_ffn_rb1': _L0_ffn_in['rb1'], 'L0_ffn_rw2': _L0_ffn_in['rw2'], 'L0_ffn_rb2': _L0_ffn_in['rb2'], 'L1_attn_Wq': _L1_attn_in['Wq'], 'L1_attn_bq': _L1_attn_in['bq'], 'L1_attn_Wk': _L1_attn_in['Wk'], 'L1_attn_bk': _L1_attn_in['bk'], 'L1_attn_Wv': _L1_attn_in['Wv'], 'L1_attn_bv': _L1_attn_in['bv'], 'L1_attn_Wo': _L1_attn_in['Wo'], 'L1_attn_bo': _L1_attn_in['bo'], 'L1_ffn_router_w': _L1_ffn_in['router_w'], 'L1_ffn_correction_bias': _L1_ffn_in['correction_bias'], 'L1_ffn_up_w': _L1_ffn_in['up_w'], 'L1_ffn_down_w': _L1_ffn_in['down_w'], 'L1_ffn_shared_up_w': _L1_ffn_in['shared_up_w'], 'L1_ffn_shared_down_w': _L1_ffn_in['shared_down_w'], 'L2_attn_ln_w': _L2_attn_in['ln_w'], 'L2_attn_ln_b': _L2_attn_in['ln_b'], 'L2_attn_Wq': _L2_attn_in['Wq'], 'L2_attn_Wk': _L2_attn_in['Wk'], 'L2_attn_Wv': _L2_attn_in['Wv'], 'L2_attn_conv_q': _L2_attn_in['conv_q'], 'L2_attn_conv_k': _L2_attn_in['conv_k'], 'L2_attn_conv_v': _L2_attn_in['conv_v'], 'L2_attn_Wb': _L2_attn_in['Wb'], 'L2_attn_Wa': _L2_attn_in['Wa'], 'L2_attn_A_log': _L2_attn_in['A_log'], 'L2_attn_dt_bias': _L2_attn_in['dt_bias'], 'L2_attn_Wg': _L2_attn_in['Wg'], 'L2_attn_norm_w': _L2_attn_in['norm_w'], 'L2_attn_Wo': _L2_attn_in['Wo'], 'L2_ffn_gate_w': _L2_ffn_in['gate_w'], 'L2_ffn_gate_b': _L2_ffn_in['gate_b'], 'L2_ffn_w1': _L2_ffn_in['w1'], 'L2_ffn_b1': _L2_ffn_in['b1'], 'L2_ffn_w2': _L2_ffn_in['w2'], 'L2_ffn_b2': _L2_ffn_in['b2'], 'L3_attn_Wq': _L3_attn_in['Wq'], 'L3_attn_Wk': _L3_attn_in['Wk'], 'L3_attn_Wv': _L3_attn_in['Wv'], 'L3_attn_Wo': _L3_attn_in['Wo'], 'L3_attn_bo': _L3_attn_in['bo'], 'L3_attn_rel_pos_bias': _L3_attn_in['rel_pos_bias'], 'L3_ffn_w_gate': _L3_ffn_in['w_gate'], 'L3_ffn_w_up': _L3_ffn_in['w_up'], 'L3_ffn_w_down': _L3_ffn_in['w_down']}
    _x0 = _d['L0_attn_inputs']
    _d['L0_attn_inputs'] = jax.random.normal(jax.random.fold_in(jax.random.key(seed), 1), (8, 512, 128), dtype=_x0.dtype)
    del _x0
    return _d

def reference(L0_attn_inputs, L0_attn_wq0, L0_attn_wq1, L0_attn_wk0, L0_attn_wk1, L0_attn_wv, L0_attn_wo, L0_attn_l0, L0_attn_l1, L0_attn_l2, L0_attn_l3, L0_attn_ln_w, L0_attn_ln_b, L0_ffn_gate_w, L0_ffn_gate_b, L0_ffn_sw1, L0_ffn_sb1, L0_ffn_sw2, L0_ffn_sb2, L0_ffn_rw1, L0_ffn_rb1, L0_ffn_rw2, L0_ffn_rb2, L1_attn_Wq, L1_attn_bq, L1_attn_Wk, L1_attn_bk, L1_attn_Wv, L1_attn_bv, L1_attn_Wo, L1_attn_bo, L1_ffn_router_w, L1_ffn_correction_bias, L1_ffn_up_w, L1_ffn_down_w, L1_ffn_shared_up_w, L1_ffn_shared_down_w, L2_attn_ln_w, L2_attn_ln_b, L2_attn_Wq, L2_attn_Wk, L2_attn_Wv, L2_attn_conv_q, L2_attn_conv_k, L2_attn_conv_v, L2_attn_Wb, L2_attn_Wa, L2_attn_A_log, L2_attn_dt_bias, L2_attn_Wg, L2_attn_norm_w, L2_attn_Wo, L2_ffn_gate_w, L2_ffn_gate_b, L2_ffn_w1, L2_ffn_b1, L2_ffn_w2, L2_ffn_b2, L3_attn_Wq, L3_attn_Wk, L3_attn_Wv, L3_attn_Wo, L3_attn_bo, L3_attn_rel_pos_bias, L3_ffn_w_gate, L3_ffn_w_up, L3_ffn_w_down):

    def _L0_attn_ref(inputs, wq0, wq1, wk0, wk1, wv, wo, l0, l1, l2, l3, ln_w, ln_b):
        import jax, jax.numpy as jnp
        import numpy as np
        B, S, D, H = (2, 256, 128, 16)
        DH = D // H
        LAMBDA_INIT = 0.8
        EPS = 1e-05

        def _forward(inputs, wq0, wq1, wk0, wk1, wv, wo, l0, l1, l2, l3, ln_w, ln_b):
            b, s, d = inputs.shape

            def proj(w):
                return jnp.einsum('bsd,de->bse', inputs, w).reshape(b, s, H, DH).transpose(0, 2, 1, 3)
            q0, q1 = (proj(wq0), proj(wq1))
            k0, k1 = (proj(wk0), proj(wk1))
            v = proj(wv)
            scale = jax.lax.rsqrt(jnp.float32(DH))
            slopes = 2.0 ** (-8.0 * jnp.arange(1, H + 1, dtype=jnp.float32) / H)
            pos = jnp.arange(s, dtype=jnp.float32)
            pos_diff = pos[:, None] - pos[None, :]
            bias = slopes[None, :, None, None] * pos_diff[None, None, :, :]
            causal = jnp.where(jnp.triu(jnp.ones((s, s), bool), 1), -jnp.inf, 0.0)[None, None]
            s0 = jnp.einsum('bhqd,bhkd->bhqk', q0, k0) * scale - bias + causal
            s1 = jnp.einsum('bhqd,bhkd->bhqk', q1, k1) * scale - bias + causal
            w0 = jax.nn.softmax(s0, axis=-1)
            w1 = jax.nn.softmax(s1, axis=-1)
            lamb = -jnp.exp(jnp.dot(l0, l1)) + LAMBDA_INIT + (-jnp.exp(jnp.dot(l2, l3)) + LAMBDA_INIT)
            diff_weights = w0 - lamb * w1
            heads = jnp.einsum('bhqk,bhkd->bhqd', diff_weights, v).transpose(0, 2, 1, 3)
            mu = jnp.mean(heads, axis=-1, keepdims=True)
            var = jnp.mean((heads - mu) ** 2, axis=-1, keepdims=True)
            normed = (heads - mu) * jax.lax.rsqrt(var + EPS) * ln_w[None, None] + ln_b[None, None]
            attention = normed.reshape(b, s, H * DH)
            return jnp.einsum('bse,ed->bsd', attention, wo)
        return _forward(inputs, wq0, wq1, wk0, wk1, wv, wo, l0, l1, l2, l3, ln_w, ln_b)

    def _L0_ffn_ref(x, gate_w, gate_b, sw1, sb1, sw2, sb2, rw1, rb1, rw2, rb2):
        import jax, jax.numpy as jnp
        import numpy as np
        B, S, D, F, O = (4, 256, 128, 512, 128)
        E, NS, K = (4, 2, 2)
        weights = jax.nn.softmax(x @ gate_w + gate_b, axis=-1)
        topk_w, topk_i = jax.lax.top_k(weights, K)
        sh = jax.nn.relu(jnp.einsum('bsd,ndf->bsnf', x, sw1) + sb1)
        shared = (jnp.einsum('bsnf,nfo->bsno', sh, sw2) + sb2).sum(axis=2) / NS
        rh = jax.nn.relu(jnp.einsum('bsd,edf->bsef', x, rw1) + rb1)
        eo = jnp.einsum('bsef,efo->bseo', rh, rw2) + rb2
        gathered = jnp.take_along_axis(eo, topk_i[..., None], axis=2)
        routed = (gathered * topk_w[..., None]).sum(axis=2)
        return shared + routed

    def _L1_attn_ref(x, Wq, bq, Wk, bk, Wv, bv, Wo, bo):
        import jax, jax.numpy as jnp
        import numpy as np
        B, L, D = (2, 256, 128)
        H = 16
        DH = D // H
        FACTOR = 0.6
        U = max(1, min(L, int(FACTOR * L)))

        def _split_heads(x):
            b, l, d = x.shape
            return x.reshape(b, l, H, DH).transpose(0, 2, 1, 3)
        b, l, _ = x.shape
        scale = 1.0 / jnp.sqrt(jnp.asarray(DH, dtype=x.dtype))
        q = _split_heads(x @ Wq + bq)
        k = _split_heads(x @ Wk + bk)
        v = _split_heads(x @ Wv + bv)
        scores = jnp.einsum('bhqd,bhkd->bhqk', q, k) * scale
        sparsity = scores.max(axis=-1) - scores.mean(axis=-1)
        _, top_idx = jax.lax.top_k(sparsity, U)
        q_sel = jnp.take_along_axis(q, top_idx[..., None], axis=2)
        scores_sel = jnp.einsum('bhud,bhkd->bhuk', q_sel, k) * scale
        attn = jax.nn.softmax(scores_sel, axis=-1)
        out_sel = jnp.einsum('bhuk,bhkd->bhud', attn, v)
        bi = jnp.arange(b)[:, None, None]
        hi = jnp.arange(H)[None, :, None]
        out = jnp.zeros_like(q).at[bi, hi, top_idx].set(out_sel)
        out = out.transpose(0, 2, 1, 3).reshape(b, l, D)
        return out @ Wo + bo

    def _L1_ffn_ref(x, router_w, correction_bias, up_w, down_w, shared_up_w, shared_down_w):
        import jax, jax.numpy as jnp
        import numpy as np
        H = 128
        E = 64
        K = 8
        G = 8
        TOPK_GROUP = 4
        I_MOE = 64
        I_SHARED = 256
        SCALE = 2.5

        def relu2(x):
            return jnp.square(jax.nn.relu(x))

        def _route(xf, router_w, correction_bias):
            T = xf.shape[0]
            logits = xf @ router_w.T
            scores = jax.nn.sigmoid(logits)
            sfc = scores + correction_bias[None, :]
            grp = sfc.reshape(T, G, E // G)
            top2, _ = jax.lax.top_k(grp, 2)
            group_scores = top2.sum(-1)
            _, gidx = jax.lax.top_k(group_scores, TOPK_GROUP)
            gmask = jnp.zeros((T, G), sfc.dtype).at[jnp.arange(T)[:, None], gidx].set(1.0)
            emask = jnp.repeat(gmask, E // G, axis=1)
            masked = jnp.where(emask > 0, sfc, 0.0)
            _, tidx = jax.lax.top_k(masked, K)
            tw = jnp.take_along_axis(scores, tidx, axis=1)
            tw = tw / (tw.sum(-1, keepdims=True) + 1e-20)
            return (tidx, tw * SCALE)
        B, S, Hd = x.shape
        xf = x.reshape(-1, Hd)
        T = xf.shape[0]
        tidx, tw = _route(xf.astype(jnp.float32), router_w, correction_bias)
        combine = jnp.zeros((T, E), xf.dtype).at[jnp.arange(T)[:, None], tidx].add(tw.astype(xf.dtype))

        def body(acc, ew):
            wu, wd, c = ew
            return (acc + c[:, None] * (relu2(xf @ wu) @ wd), None)
        routed, _ = jax.lax.scan(body, jnp.zeros_like(xf), (up_w, down_w, combine.T))
        shared = relu2(xf @ shared_up_w) @ shared_down_w
        return (routed + shared).reshape(B, S, Hd)

    def _L2_attn_ref(x, ln_w, ln_b, Wq, Wk, Wv, conv_q, conv_k, conv_v, Wb, Wa, A_log, dt_bias, Wg, norm_w, Wo):
        import jax, jax.numpy as jnp
        import numpy as np
        D = 128
        H = 4
        DK = D
        DV = 2 * D
        HK = DK // H
        HV = DV // H
        KCONV = 4
        EPS = 1e-05
        CHUNK = 64

        def causal_conv_silu(x, w):
            B, T, C = x.shape
            K = w.shape[1]
            xp = jnp.pad(x, ((0, 0), (K - 1, 0), (0, 0)))
            y = sum((xp[:, i:i + T, :] * w[:, i] for i in range(K)))
            return jax.nn.silu(y)

        def l2norm(x):
            return x * jax.lax.rsqrt(jnp.sum(x * x, -1, keepdims=True) + 1e-06)

        def _step(S, inp):
            q_t, k_t, v_t, g_t, b_t = inp
            S = S * jnp.exp(g_t)[..., None, None]
            v_eff = (v_t - jnp.einsum('bhk,bhkv->bhv', k_t, S)) * b_t[..., None]
            S = S + k_t[..., None] * v_eff[..., None, :]
            o_t = jnp.einsum('bhk,bhkv->bhv', q_t, S)
            return (S, o_t)

        @jax.checkpoint
        def _chunk(S, ch):
            return jax.lax.scan(_step, S, ch)

        def _forward(x, ln_w, ln_b, Wq, Wk, Wv, conv_q, conv_k, conv_v, Wb, Wa, A_log, dt_bias, Wg, norm_w, Wo):
            B, T, _ = x.shape
            mu = jnp.mean(x, -1, keepdims=True)
            var = jnp.mean((x - mu) ** 2, -1, keepdims=True)
            normed = (x - mu) * jax.lax.rsqrt(var + EPS) * ln_w + ln_b
            q = causal_conv_silu(normed @ Wq, conv_q)
            k = causal_conv_silu(normed @ Wk, conv_k)
            v = causal_conv_silu(normed @ Wv, conv_v)
            beta = jax.nn.sigmoid(normed @ Wb)
            g = -jnp.exp(A_log) * jax.nn.softplus(normed @ Wa + dt_bias)
            q = l2norm(q.reshape(B, T, H, HK)) * HK ** (-0.5)
            k = l2norm(k.reshape(B, T, H, HK))
            v = v.reshape(B, T, H, HV)
            nc = T // CHUNK

            def to_chunks(a):
                return jnp.moveaxis(a, 1, 0).reshape((nc, CHUNK, B) + a.shape[2:])
            qc, kc, vc, gc, bc = map(to_chunks, (q, k, v, g, beta))
            S0 = jnp.zeros((B, H, HK, HV), x.dtype)
            _, o = jax.lax.scan(_chunk, S0, (qc, kc, vc, gc, bc))
            o = jnp.moveaxis(o.reshape(T, B, H, HV), 0, 1)
            g_out = (normed @ Wg).reshape(B, T, H, HV)
            o = o * jax.lax.rsqrt(jnp.mean(o * o, -1, keepdims=True) + EPS) * norm_w
            o = o * g_out * jax.nn.sigmoid(g_out)
            return x + o.reshape(B, T, DV) @ Wo
        return _forward(x, ln_w, ln_b, Wq, Wk, Wv, conv_q, conv_k, conv_v, Wb, Wa, A_log, dt_bias, Wg, norm_w, Wo)

    def _L2_ffn_ref(x, gate_w, gate_b, w1, b1, w2, b2):
        import jax, jax.numpy as jnp
        import numpy as np
        D_MODEL = 128
        FF = 512
        E = 8
        TOP_K = 2
        CAP_FACTOR = 1.25
        B, T = (4, 256)

        def _moe_forward(x, gate_w, gate_b, w1, b1, w2, b2):
            Bb, Tt, d = x.shape
            S = Bb * Tt
            C = int(CAP_FACTOR * S / E)
            xf = x.reshape(S, d)
            logits = xf @ gate_w + gate_b
            probs = jax.nn.softmax(logits, axis=1)
            topk_p, topk_i = jax.lax.top_k(probs, TOP_K)
            topk_pn = topk_p / jnp.sum(topk_p, axis=1, keepdims=True)
            rows = jnp.arange(S)
            w_te = jnp.zeros((S, E), xf.dtype).at[rows[:, None], topk_i].set(topk_pn)
            mask = jnp.zeros((S, E), bool).at[rows[:, None], topk_i].set(True)
            rank = jnp.cumsum(mask.astype(jnp.int32), axis=0)
            slot = jnp.where(mask & (rank <= C), rank - 1, C)
            e_grid = jnp.broadcast_to(jnp.arange(E), (S, E))
            t_grid = jnp.broadcast_to(rows[:, None], (S, E))
            buf = jnp.full((E, C + 1), S, jnp.int32).at[e_grid, slot].set(t_grid)
            idx = buf[:, :C]
            valid = idx < S
            x_pad = jnp.concatenate([xf, jnp.zeros((1, d), xf.dtype)], axis=0)
            xin = x_pad[idx]
            h = jax.nn.relu(jnp.einsum('ecd,edh->ech', xin, w1) + b1[:, None, :])
            out = jnp.einsum('ech,ehd->ecd', h, w2) + b2[:, None, :]
            w_pad = jnp.concatenate([w_te, jnp.zeros((1, E), xf.dtype)], axis=0)
            tok_w = w_pad[idx, jnp.arange(E)[:, None]]
            out = out * jnp.where(valid, tok_w, 0.0)[:, :, None]
            final = jnp.zeros((S + 1, d), xf.dtype).at[idx.reshape(-1)].add(out.reshape(-1, d))[:S]
            return final.reshape(Bb, Tt, d)
        return _moe_forward(x, gate_w, gate_b, w1, b1, w2, b2)

    def _L3_attn_ref(x, Wq, Wk, Wv, Wo, bo, rel_pos_bias):
        import jax, jax.numpy as jnp
        import numpy as np
        N_HEADS = 16
        D_MODEL = 128
        D_HEAD = 64
        MAX_SEQ_LEN = 128

        def _pos_bias(rel_pos_bias, T):
            i = jnp.arange(T)[:, None]
            j = jnp.arange(T)[None, :]
            idx = jnp.clip(MAX_SEQ_LEN - 1 - (i - j), 0, MAX_SEQ_LEN - 1)
            bias = rel_pos_bias[:, idx]
            return jnp.where((j <= i)[None], bias, 0.0)
        B, T, _ = x.shape
        H, dh = (N_HEADS, D_HEAD)
        q = (x @ Wq).reshape(B, T, H, dh).transpose(0, 2, 1, 3)
        k = (x @ Wk).reshape(B, T, H, dh).transpose(0, 2, 1, 3)
        v = (x @ Wv).reshape(B, T, H, dh).transpose(0, 2, 1, 3)
        logits = jnp.einsum('bhqd,bhkd->bhqk', q, k)
        i = jnp.arange(T)[:, None]
        j = jnp.arange(T)[None, :]
        causal = jnp.where(j > i, -jnp.inf, 0.0)
        logits = logits + causal[None, None] + _pos_bias(rel_pos_bias, T)[None]
        logits = logits / dh
        probs = jax.nn.softmax(logits, axis=-1)
        out = jnp.einsum('bhqk,bhkd->bhqd', probs, v)
        out = out.transpose(0, 2, 1, 3).reshape(B, T, H * dh)
        return out @ Wo + bo

    def _L3_ffn_ref(x, w_gate, w_up, w_down):
        import jax, jax.numpy as jnp
        import numpy as np
        DIM = 128
        HIDDEN = 384
        SCALE = 1.0 / 127.0

        def _dequant(w_int, dtype):
            return w_int.astype(dtype) * jnp.asarray(SCALE, dtype)
        wg = _dequant(w_gate, x.dtype)
        wu = _dequant(w_up, x.dtype)
        wd = _dequant(w_down, x.dtype)
        gate = jnp.einsum('bsd,hd->bsh', x, wg)
        up = jnp.einsum('bsd,hd->bsh', x, wu)
        h = jax.nn.silu(gate) * up
        return jnp.einsum('bsh,dh->bsd', h, wd)
    x = L0_attn_inputs
    xn = _layernorm(x, axis=-1)
    s = _L0_attn_ref(xn, L0_attn_wq0, L0_attn_wq1, L0_attn_wk0, L0_attn_wk1, L0_attn_wv, L0_attn_wo, L0_attn_l0, L0_attn_l1, L0_attn_l2, L0_attn_l3, L0_attn_ln_w, L0_attn_ln_b)
    g = _silu(_L0_ffn_ref(xn, L0_ffn_gate_w, L0_ffn_gate_b, L0_ffn_sw1, L0_ffn_sb1, L0_ffn_sw2, L0_ffn_sb2, L0_ffn_rw1, L0_ffn_rb1, L0_ffn_rw2, L0_ffn_rb2))
    x = x + s * g
    xn = _layernorm(x, axis=-1)
    s = _L1_attn_ref(xn, L1_attn_Wq, L1_attn_bq, L1_attn_Wk, L1_attn_bk, L1_attn_Wv, L1_attn_bv, L1_attn_Wo, L1_attn_bo)
    g = _silu(_L1_ffn_ref(xn, L1_ffn_router_w, L1_ffn_correction_bias, L1_ffn_up_w, L1_ffn_down_w, L1_ffn_shared_up_w, L1_ffn_shared_down_w))
    x = x + s * g
    xn = _layernorm(x, axis=-1)
    s = _L2_attn_ref(xn, L2_attn_ln_w, L2_attn_ln_b, L2_attn_Wq, L2_attn_Wk, L2_attn_Wv, L2_attn_conv_q, L2_attn_conv_k, L2_attn_conv_v, L2_attn_Wb, L2_attn_Wa, L2_attn_A_log, L2_attn_dt_bias, L2_attn_Wg, L2_attn_norm_w, L2_attn_Wo)
    g = _silu(_L2_ffn_ref(xn, L2_ffn_gate_w, L2_ffn_gate_b, L2_ffn_w1, L2_ffn_b1, L2_ffn_w2, L2_ffn_b2))
    x = x + s * g
    xn = _layernorm(x, axis=-1)
    s = _L3_attn_ref(xn, L3_attn_Wq, L3_attn_Wk, L3_attn_Wv, L3_attn_Wo, L3_attn_bo, L3_attn_rel_pos_bias)
    g = _silu(_L3_ffn_ref(xn, L3_ffn_w_gate, L3_ffn_w_up, L3_ffn_w_down))
    x = x + s * g
    return x

_drawn_inputs = setup_inputs


def setup_inputs(seed=0):
    import zlib

    import numpy as np

    out = dict(_drawn_inputs(seed))
    spreads = {'L0_attn_ln_w': (1.0, 0.2),
     'L0_attn_ln_b': (0.0, 0.1),
     'L0_ffn_gate_b': (0.0, 0.416),
     'L0_ffn_sb1': (0.0, 0.425),
     'L0_ffn_sb2': (0.0, 0.1),
     'L0_ffn_rb1': (0.0, 0.631),
     'L0_ffn_rb2': (0.0, 0.344),
     'L1_attn_bq': (0.0, 0.8),
     'L1_attn_bk': (0.0, 2.0),
     'L1_attn_bv': (0.0, 0.8),
     'L1_attn_bo': (0.0, 0.8),
     'L2_attn_ln_w': (1.0, 0.6),
     'L2_attn_ln_b': (0.0, 0.8),
     'L2_attn_norm_w': (1.0, 0.6),
     'L2_ffn_gate_b': (0.0, 0.1),
     'L2_ffn_b1': (0.0, 0.623),
     'L2_ffn_b2': (0.0, 0.1),
     'L3_attn_bo': (0.0, 0.1)}
    factors = {'L0_attn_wq0': 8.0,
     'L0_attn_wq1': 8.0,
     'L0_attn_wk0': 8.0,
     'L0_attn_wk1': 8.0,
     'L0_attn_l0': 8.0,
     'L0_attn_l1': 8.0,
     'L0_attn_l2': 8.0,
     'L0_attn_l3': 8.0,
     'L1_attn_Wq': 8.0,
     'L1_attn_Wk': 8.0,
     'L1_attn_Wv': 8.0,
     'L1_attn_Wo': 8.0,
     'L1_ffn_router_w': 8.0,
     'L1_ffn_correction_bias': 8.0,
     'L1_ffn_up_w': 8.0,
     'L1_ffn_down_w': 8.0,
     'L1_ffn_shared_up_w': 8.0,
     'L1_ffn_shared_down_w': 8.0,
     'L2_attn_Wq': 8.0,
     'L2_attn_Wk': 8.0,
     'L2_attn_Wv': 8.0,
     'L2_attn_conv_q': 8.0,
     'L2_attn_conv_k': 8.0,
     'L2_attn_conv_v': 8.0,
     'L2_attn_Wb': 8.0,
     'L2_attn_Wa': 55.407,
     'L2_attn_A_log': 21.44,
     'L2_attn_dt_bias': 23.162,
     'L2_attn_Wg': 8.0,
     'L2_attn_Wo': 8.0,
     'L3_attn_rel_pos_bias': 64.0}
    for name, (base, spread) in spreads.items():
        noise = np.random.default_rng([zlib.crc32(name.encode()), seed]).standard_normal(out[name].shape)
        drawn = base * np.exp(spread * noise) if base else spread * noise
        out[name] = jnp.asarray(drawn.astype(out[name].dtype))
    for name, factor in factors.items():
        out[name] = (out[name] * factor).astype(out[name].dtype)
    return out
```

```python
from contextlib import ExitStack, contextmanager

import numpy as np

import concourse.bass as bass
from concourse import mybir

P = 128
D = 128
B, T = 8, 512
NT = B * T // P
QT = T // P
EPS = 1e-5

ALU = mybir.AluOpType
ACT = mybir.ActivationFunctionType
AX = mybir.AxisListType
F32 = mybir.dt.float32
BF16 = mybir.dt.bfloat16
I32 = mybir.dt.int32


class Phase:

    def __init__(self, nc, ctx, name, tail):
        self.nc, self.ctx, self.name, self.sems, self.tail = nc, ctx, name, [], tail

    def sb(self, name, shape, dt=F32):
        return self.ctx.enter_context(self.nc.sbuf_tensor(f"{self.name}_{name}", shape, dt))

    def ps(self, name, shape, dt=F32):
        return self.ctx.enter_context(self.nc.psum_tensor(f"{self.name}_{name}", shape, dt))

    def sem(self, name):
        s = self.ctx.enter_context(self.nc.semaphore(f"{self.name}_{name}"))
        self.sems.append(s)
        return s


@contextmanager
def phase(nc, name):
    with ExitStack() as ctx:
        p = Phase(nc, ctx, name, None)
        yield p
        nums = sorted(s.num for s in p.sems)
        if nums:
            with nc.Block() as block:
                @block.gpsimd
                def _(pool):
                    starts = [n for n in nums if n - 1 not in nums]
                    for a in starts:
                        pool.sem_clear(range(a, next(n for n in range(a, a + len(nums) + 1) if n not in nums)))


def scaled(eng, n, per, plus=0):
    if isinstance(n, int):
        return n * per + plus
    return eng.snap(n * per + plus)


class Chain:

    def __init__(self, eng, sem, per):
        self.eng, self.sem, self.per, self.k = eng, sem, per, 0

    def step(self, n):
        self.base, self.k = scaled(self.eng, n, self.per), 0

    def did(self, ins):
        self.k += 1
        return ins.then_inc(self.sem, 1)

    def wait(self):
        self.eng.wait_ge(self.sem, self.base + self.k)

    def link(self, ins):
        self.did(ins)
        self.wait()

    def over(self):
        assert self.k == self.per, (self.k, self.per)


def norm_phase(nc, R, name, combine, second=None, store=None):
    with phase(nc, name) as p:
        NV = 2 if second else 1
        per = (QT + 1) * NV + (2 if combine else 0)
        ex = p.sb("ex", [P, 2, T])
        xn = p.sb("xn", [P, 2, QT, D])
        xm = p.sb("xm", [P, 2, QT, D])
        stats = p.sb("stats", [P, 2, QT, 6])
        mv = p.sb("mv", [P, 2, QT, 2])
        ve = p.sb("ve", [P, 2, QT])
        rs = p.sb("rs", [P, 2, QT])
        half = p.sb("half", [P, QT])
        pT = p.ps("pT", [P, 2, T])
        s_half = p.sem("half")
        s_exp = p.sem("exp")
        s_dve = p.sem("dve")
        s_var = p.sem("var")
        s_rs = p.sem("rs")
        s_xn = p.sem("xn")
        s_pT = p.sem("pT")
        s_xT = p.sem("xT")
        with nc.Block() as block:
            @block.gpsimd
            def _(pool):
                nc.gpsimd.memset(half[:, :], -0.5).then_inc(s_half, 1)
                pool.wait_ge(s_half, 1)
                with pool.Fori(0, B // 2) as i:
                    for u in range(2):
                        n = i * 2 + u
                        for v in range(NV):
                            pool.wait_ge(s_var, scaled(pool, n, NV, v + 1))
                            nc.gpsimd.tensor_tensor(rs[:, u], ve[:, u], half[:, :], ALU.pow).then_inc(s_rs, 1)

            @block.scalar
            def _(act):
                def body(i, first, last):
                    if combine:
                        for u in range(2):
                            n = i * 2 + u
                            if not first:
                                act.wait_ge(s_dve, scaled(act, i, 2 * per))
                            nc.scalar.activation(ex[:, u], R.f[:, bass.ds(n * QT, QT), :].rearrange("p a d -> p (a d)"),
                                                 ACT.Silu).then_inc(s_exp, 1)
                    for u in range(2):
                        n = i * 2 + u
                        for v in range(NV):
                            act.wait_ge(s_pT, scaled(act, n, NV, v + 1))
                            if v == 0:
                                nc.scalar.activation(R.xnT[:, bass.ds(n * T, T)], pT[:, (v + u * NV) % 2], ACT.Copy).then_inc(s_xT, 1)
                            else:
                                nc.scalar.activation(R.xn2T[:, bass.ds(n * T, T)], pT[:, (v + u * NV) % 2], ACT.Identity,
                                                     bias=second[1], scale=second[0]).then_inc(s_xT, 1)

                run_bodies(act, B // 2, body)

            @block.tensor
            def _(pe):
                def body(i, first, last):
                    for u in range(2):
                        n = i * 2 + u
                        for v in range(NV):
                            pe.wait_ge(s_xn, scaled(pe, n, NV, v + 1))
                            if not (first and u * NV + v < 2):
                                pe.wait_ge(s_xT, scaled(pe, n, NV, v - 1))
                            for j in range(QT):
                                ins = nc.tensor.transpose(pT[:, (v + u * NV) % 2, j * P:(j + 1) * P],
                                                          (xm if v else xn)[:, u, j], R.ident[:, :])
                            ins.then_inc(s_pT, 1)

                run_bodies(pe, B // 2, body)

            @block.vector
            def _(dve):
                c = Chain(dve, s_dve, per)

                def body(i, first, last):
                    for u in range(2):
                        n = i * 2 + u
                        c.step(n)
                        xb = R.x[:, bass.ds(n * QT, QT), :]
                        if combine:
                            e, fb = ex[:, u], R.f[:, bass.ds(n * QT, QT), :].rearrange("p a d -> p (a d)")
                            sb_ = R.s[:, bass.ds(n * QT, QT), :].rearrange("p a d -> p (a d)")
                            xf = xb.rearrange("p a d -> p (a d)")
                            dve.wait_ge(s_exp, n + 1)
                            c.link(nc.vector.tensor_tensor(e, e, sb_, ALU.mult))
                            c.did(nc.vector.tensor_tensor(xf, e, xf, ALU.add))
                        for v in range(NV):
                            dve.drain()
                            for j in range(QT):
                                src = R.x[:, bass.ds(n * QT + j, 1), :].rearrange("p a d -> p (a d)") if v == 0 else xn[:, u, j]
                                nc.vector.bn_stats(stats[:, u, j], src)
                            dve.drain()
                            for j in range(QT):
                                c.did(nc.vector.bn_aggr(mv[:, u, j], stats[:, u, j]))
                            c.wait()
                            nc.vector.tensor_scalar(ve[:, u], mv[:, u, :, 1], EPS, None, ALU.add).then_inc(s_var, 1)
                            dst = xm if v else xn
                            if v == 0:
                                src = xb
                                if not first:
                                    dve.wait_ge(s_pT, scaled(dve, i, 2 * NV))
                            else:
                                src = xn[:, u]
                            c.link(nc.vector.tensor_tensor(dst[:, u], src, mv[:, u, :, 0:1].broadcast_to([P, QT, D]), ALU.subtract))
                            dve.wait_ge(s_rs, scaled(dve, n, NV, v + 1))
                            nc.vector.tensor_tensor(dst[:, u], dst[:, u], rs[:, u].rearrange("p (a o) -> p a o", o=1).broadcast_to([P, QT, D]),
                                                    ALU.mult).then_inc(s_xn, 1)
                            if v == 0 and (store is not None or second):
                                dve.wait_ge(s_xn, scaled(dve, n, NV, v + 1))
                            if v == 0 and store is not None:
                                dve.nop(nofuse=True)
                                nc.vector.tensor_copy(store[:, bass.ds(n * QT, QT), :], xn[:, u])
                        c.over()

                run_bodies(dve, B // 2, body)


class At:

    def __init__(self, eng, i):
        self.eng, self.i, self.bases = eng, i, {}

    def __call__(self, per, plus):
        if isinstance(self.i, int):
            return self.i * per + plus
        if per not in self.bases:
            self.bases[per] = self.eng.snap(self.i * per)
        return self.bases[per] + plus


def run_bodies(eng, count, body):
    body(0, True, False)
    with eng.Fori(1, count - 1) as i:
        body(i, False, False)
    body(count - 1, False, True)


NH, DH = 16, 8
STACK = 9 * DH


def project_phase(nc, R, name, wqk, bqk, wv, bv, parts, vtok, qscale=None, mean=None):
    M2 = len(wqk)
    with phase(nc, name) as p:
        w = p.sb("w", [P, M2 + 1, P])
        bias = p.sb("bias", [P, M2 + 1])
        full = p.sb("full", [P, 2, T])
        rest = p.sb("rest", [P, 2, T])
        part = p.sb("part", [P, 4, 3, T], BF16)
        vT = p.sb("vT", [P, 2, T])
        ps = p.ps("ps", [P, 2, T])
        pv = p.ps("pv", [P, 2, T])
        pvt = p.ps("pvt", [P, 2, T])
        pm = p.ps("pm", [P, 2, T]) if mean is not None else None
        s_w = p.sem("w")
        s_mm = p.sem("mm")
        s_full = p.sem("full")
        s_split = p.sem("split")
        s_put = [p.sem(f"put{k}") for k in range(4)]
        s_vmm = p.sem("vmm")
        s_vT = p.sem("vT")
        s_vt = p.sem("vt")
        s_v = p.sem("v")
        nw = M2 + 1 + 2
        if qscale is not None:
            qsc = p.sb("qsc", [P, 1])
            nw += 1
        if mean is not None:
            qf = p.sb("qf", [P, 2, T])
            kbar = p.sb("kbar", [P, 2, 1])
            kblk = p.sb("kblk", [P, 2, NH])
            hmask = p.sb("hmask", [P, NH])
            s_qf = p.sem("qf")
            s_kblk = p.sem("kblk")
            s_mean = p.sem("mean")
            s_mcp = p.sem("mcp")
            nw += 1
        NBODY = B // 2
        with nc.Block() as block:
            @block.sync
            def _(sp):
                for m in range(M2):
                    sp.dma_start(w[:, m], wqk[m]).then_inc(s_w, 16)
                sp.dma_start(w[:, M2], wv).then_inc(s_w, 16)
                sp.dma_start(bias[:, :M2], bqk).then_inc(s_w, 16)
                sp.dma_start(bias[:, M2:], bv).then_inc(s_w, 16)
                if qscale is not None:
                    sp.dma_start(qsc[:, :], qscale).then_inc(s_w, 16)
                if mean is not None:
                    sp.dma_start(hmask[:, :], mean["hmask"]).then_inc(s_w, 16)
                with sp.Fori(0, NBODY) as i:
                    at = At(sp, i)
                    for g in range(2 * M2):
                        u, m = divmod(g, M2)
                        sp.wait_ge(s_split, at(2 * M2, g + 1))
                        for k in range(3):
                            dst = parts[m % 2, bass.ds((i * 2 + u) * NH, NH), m // 2, 2 - k if m % 2 else k, :, :]
                            sp.dma_start(dst, part[:, g % 4, k]).then_inc(s_put[g % 4], 16)
                for s in s_put:
                    sp.wait_ge(s, 12 * M2 * B)

            @block.tensor
            def _(pe):
                pe.wait_ge(s_w, 16 * nw)

                def body(i, first, last):
                    at = At(pe, i)
                    for u in range(2):
                        xb = R.xnT[:, bass.ds((i * 2 + u) * T, T)]
                        for m in range(M2):
                            g = u * M2 + m
                            if not (first and g < 2):
                                pe.wait_ge(s_full, at(2 * M2, g - 1))
                            nc.tensor.matmul(ps[:, g % 2], w[:, m], xb, start=True, stop=True).then_inc(s_mm, 1)
                        if not (first and u == 0):
                            pe.wait_ge(s_vT, at(2, u))
                        nc.tensor.matmul(pv[:, 0], w[:, M2], xb, start=True, stop=True).then_inc(s_vmm, 1)
                        pe.wait_ge(s_vT, at(2, u + 1))
                        if not first:
                            pe.wait_ge(s_v, at(2, u - 1))
                        for j in range(QT):
                            ins = nc.tensor.transpose(pvt[:, u, j * P:(j + 1) * P], vT[:, u, j * P:(j + 1) * P], R.ident[:, :])
                        ins.then_inc(s_vt, 1)
                        if mean is not None:
                            pe.wait_ge(s_qf, at(2, u + 1))
                            pe.wait_ge(s_kblk, at(2, u + 1))
                            if not first:
                                pe.wait_ge(s_mcp, at(2, u - 1))
                            for j in range(QT):
                                ins = nc.tensor.matmul(pm[:, u, j * NH:(j + 1) * NH], qf[:, u, j * P:(j + 1) * P], kblk[:, u, :], start=True, stop=True)
                            ins.then_inc(s_mean, 1)

                run_bodies(pe, NBODY, body)

            @block.scalar
            def _(act):
                act.wait_ge(s_w, 16 * nw)

                def body(i, first, last):
                    at = At(act, i)
                    for u in range(2):
                        for m in range(M2):
                            g = u * M2 + m
                            act.wait_ge(s_mm, at(2 * M2, g + 1))
                            if not (first and g < 2):
                                act.wait_ge(s_split, at(2 * M2, g - 1))
                            if mean is not None and m == 0:
                                if not first:
                                    act.wait_ge(s_mean, at(2, u - 1))
                                nc.scalar.activation(qf[:, u], ps[:, g % 2], ACT.Identity, bias=bias[:, m:m + 1]).then_inc(s_qf, 1)
                            if not (first and g < 4):
                                act.wait_ge(s_put[g % 4], at(M2 * 24, 48 * (g // 4)))
                            for dst in (full[:, g % 2], part[:, g % 4, 0]):
                                ins = nc.scalar.activation(dst, ps[:, g % 2], ACT.Identity, bias=bias[:, m:m + 1],
                                                           scale=qsc[:, 0:1] if qscale is not None and m % 2 == 0 else 1.0)
                            ins.then_inc(s_full, 1)
                        act.wait_ge(s_vmm, at(2, u + 1))
                        if not first:
                            act.wait_ge(s_vt, at(2, u - 1))
                        nc.scalar.activation(vT[:, u], pv[:, 0], ACT.Identity, bias=bias[:, M2:M2 + 1]).then_inc(s_vT, 1)
                        act.wait_ge(s_vt, at(2, u + 1))
                        nc.scalar.activation(vtok[:, bass.ds((i * 2 + u) * NH, NH), :, :DH],
                                             pvt[:, u].rearrange("p (q h d) -> p h q d", q=QT, h=NH), ACT.Copy).then_inc(s_v, 1)
                        if mean is not None:
                            act.wait_ge(s_mean, at(2, u + 1))
                            nc.scalar.activation(mean["sum"][:, bass.ds((i * 2 + u) * QT, QT), :], pm[:, u, :QT * NH].rearrange("p (q h) -> p q h", h=NH), ACT.Copy).then_inc(s_mcp, 1)

                run_bodies(act, NBODY, body)

            @block.vector
            def _(dve):
                dve.wait_ge(s_w, 16 * nw)

                def body(i, first, last):
                    at = At(dve, i)
                    for u in range(2):
                        for m in range(M2):
                            g = u * M2 + m
                            x, r1 = full[:, g % 2], rest[:, g % 2]
                            pt = part[:, g % 4]
                            dve.wait_ge(s_full, at(2 * M2, g + 1))
                            if not (first and g < 4):
                                dve.wait_ge(s_put[g % 4], at(M2 * 24, 48 * (g // 4)))
                            nc.vector.tensor_tensor(r1, x, pt[:, 0], ALU.subtract)
                            if mean is not None and m == 1:
                                nc.vector.reduce_sum(kbar[:, u], x, AX.X)
                            dve.drain()
                            if mean is not None and m == 1:
                                if not first:
                                    dve.wait_ge(s_mean, at(2, u - 1))
                                nc.vector.tensor_scalar(kblk[:, u], hmask[:, :], kbar[:, u], None, ALU.mult).then_inc(s_kblk, 1)
                            nc.vector.tensor_copy(pt[:, 1], r1)
                            dve.drain()
                            nc.vector.tensor_tensor(pt[:, 2], r1, pt[:, 1], ALU.subtract).then_inc(s_split, 1)

                run_bodies(dve, NBODY, body)


RUNS = ((0, 0, 3), (0, 1, 2), (0, 2, 1), (1, 0, 2), (2, 0, 1))


def attend_phase(nc, R, name, maps, parts, ext, gain, vtok, heads, masks=None, lamb=None, negmax=None):
    N = B * NH
    UN = 4
    GH = UN // maps
    NG = N // GH
    NB = 4
    causal = masks is not None
    NX = 4 if causal else 0
    K1, K2 = STACK + NX, STACK + NX + 3
    IT = UN * QT
    DV = DH + 1
    with phase(nc, name) as p:
        qs = p.sb("qs", [K2, NB, UN, T], BF16)
        ks = p.sb("ks", [K2, NB, UN, T], BF16)
        ex = p.sb("ex", [NX + 3, 2, T])
        exb = p.sb("exb", [NX + 3, 2, T], BF16)
        mx = p.sb("mx", [P, NB, IT])
        m0 = p.sb("m0", [IT, 3, P])
        mp = p.sb("mp", [IT, 2, 3, P], BF16)
        E = p.sb("E", [P, 2, UN, T])
        vs = p.sb("vs", [P, 2, GH, QT, DV])
        gs = p.sb("gs", [P, 2, GH])
        gains = p.sb("gains", [P, N])
        oT = p.sb("oT", [P, 2, T])
        rz = p.sb("rz", [P, QT, UN])
        o1 = p.sb("o1", [P, GH, QT, DH])
        if causal:
            mk = p.sb("mk", [P, 3, P])
            mb = p.sb("mb", [P, 3, P], BF16)
        pS = p.ps("pS", [P, 2, T])
        pX = p.ps("pX", [P, 2, T])
        pO = p.ps("pO", [P, 2, T])
        pM = p.ps("pM", [P, T])
        pT = p.ps("pT", [P, T])
        s_c, s_cb, s_ce, s_z = (p.sem(k) for k in ("c", "cb", "ce", "z"))
        s_in = [p.sem(f"in{u}") for u in range(NB)]
        s_mr = [p.sem(f"mr{u}") for u in range(NB)]
        s_p1 = p.sem("p1")
        s_mx = p.sem("mx")
        s_mt = p.sem("mt")
        s_mp = p.sem("mp")
        s_p2 = p.sem("p2")
        s_e = p.sem("e")
        s_pv = p.sem("pv")
        s_oT = p.sem("oT")
        s_tr = p.sem("tr")
        s_st = p.sem("st")
        s_vs = p.sem("vs")
        COUNT = NG // NB
        NL = 2 * len(RUNS) * 16
        w1 = lambda j: (j + 1) * P if causal else T
        q0 = lambda kt: kt * P if causal else 0
        of = lambda at, per, h, k: at(NB * per, per * h + k)

        with nc.Block() as block:
            @block.sync
            def _(sp):
                sp.dma_start(ex[:, :, :], ext).then_inc(s_c, 16)
                sp.dma_start(gains[:, :], gain).then_inc(s_c, 16)
                if causal:
                    sp.dma_start(mk[:, :, :], masks).then_inc(s_c, 16)
                sp.wait_ge(s_cb, 1)
                src = exb[:, 0:1].broadcast_to([NX + 3, NB * UN, T])
                sp.dma_start(qs[STACK:, :, :, :].rearrange("r b x t -> r (b x) t"), src).then_inc(s_ce, 16)
                src = exb[:, 1:2].broadcast_to([NX + 3, NB * UN, T])
                sp.dma_start(ks[STACK:, :, :, :].rearrange("r b x t -> r (b x) t"), src).then_inc(s_ce, 16)
                sp.wait_ge(s_ce, 32)

                def load(at, i, h, free):
                    if not free:
                        sp.wait_ge(s_p2, of(at, IT, h - NB, IT))
                    u, row = h % NB, 0
                    for a, b, many in RUNS:
                        rows = slice(row, row + many * DH)
                        for dst, side, f in ((qs, 0, a), (ks, 1, b)):
                            src = parts[side, bass.ds((i * NB + h) * GH, GH), :, f:f + many, :, :].rearrange("n m k d t -> (k d) (n m) t")
                            sp.dma_start(dst[rows, u], src).then_inc(s_in[u], 16)
                        row += many * DH

                def maxima(at, h):
                    sp.wait_ge(s_mp, of(at, 1, h, 1))
                    for k in range(3):
                        dst = qs[K1 + k:K1 + k + 1, h % NB].rearrange("r x (j q) -> r (x j) q", q=P)
                        sp.dma_start(dst, mp[:, h % 2, k]).then_inc(s_mr[h % NB], 16)

                def body(i, first, last):
                    at = At(sp, i)
                    if first:
                        load(at, i, 0, True)
                        load(at, i, 1, True)
                        maxima(at, 0)
                        load(at, i, 2, True)
                    for g in range(NB):
                        if not (last and g + 3 >= NB):
                            load(at, i, g + 3, first and g + 3 < NB)
                        if not (last and g + 1 >= NB):
                            maxima(at, g + 1)

                run_bodies(sp, COUNT, body)

            @block.gpsimd
            def _(pool):
                pool.wait_ge(s_c, 48 if causal else 32)
                nc.gpsimd.memset(vtok[:, :, :, DH:], 1.0)
                pool.drain()

                def body(i, first, last):
                    at = At(pool, i)
                    for g in range(NB):
                        if not (first and g < 2):
                            pool.wait_ge(s_pv, of(at, QT, g - 2, QT))
                        n = bass.ds((i * NB + g) * GH, GH)
                        nc.gpsimd.tensor_copy(gs[:, g % 2], gains[:, n])
                        nc.gpsimd.tensor_copy(vs[:, g % 2], vtok[:, n, :, :]).then_inc(s_vs, 1)

                run_bodies(pool, COUNT, body)

            @block.tensor
            def _(pe):
                pe.wait_ge(s_cb, 1)
                pe.wait_ge(s_ce, 32)
                pe.wait_ge(s_z, 1)

                def pass1(at, h, r, early):
                    u, (x, j) = h % NB, divmod(r, QT)
                    if r == 0:
                        pe.wait_ge(s_in[u], at(NL, NL * (h // NB + 1)))
                    if not (early and r < 2):
                        pe.wait_ge(s_mx, of(at, IT, h, r - 1))
                    w = w1(j)
                    ins = nc.tensor.matmul(pS[:, r % 2, :w], qs[:K1, u, x, j * P:(j + 1) * P], ks[:K1, u, x, :w], start=True, stop=not causal)
                    if causal:
                        ins = nc.tensor.matmul(pS[:, r % 2, w - P:w], mb[:, 2], mb[:, 0], start=False, stop=True)
                    ins.then_inc(s_p1, 1)

                def turn_maxima(at, h, early):
                    pe.wait_ge(s_mx, of(at, IT, h, IT))
                    if not early:
                        pe.wait_ge(s_mp, of(at, 1, h, 0))
                    nc.tensor.transpose(pM[:IT, :P], mx[:, h % NB], R.ident[:, :]).then_inc(s_mt, 1)

                def pass2(at, g, s, early):
                    kt, x = divmod(s, UN)
                    if s == 0:
                        pe.wait_ge(s_mr[g % NB], at(48, 48 * (g // NB + 1)))
                    if not (early and s < 2):
                        pe.wait_ge(s_e, of(at, IT, g, s - 1))
                    w = T - q0(kt)
                    ins = nc.tensor.matmul(pX[:, s % 2, :w], ks[:, g % NB, x, kt * P:(kt + 1) * P], qs[:, g % NB, x, q0(kt):], start=True, stop=not causal)
                    if causal:
                        ins = nc.tensor.matmul(pX[:, s % 2, :P], mb[:, 2], mb[:, 1], start=False, stop=True)
                    ins.then_inc(s_p2, 1)

                def weigh(at, g, kt, early):
                    if kt == 0:
                        pe.wait_ge(s_vs, of(at, 1, g, 1))
                        if not early:
                            pe.wait_ge(s_oT, of(at, 1, g, -1))
                    pe.wait_ge(s_e, of(at, IT, g, UN * (kt + 1)))
                    w = T - q0(kt)
                    for x in range(UN):
                        ins = nc.tensor.matmul(pO[32 * x:32 * x + DV, g % 2, q0(kt):], vs[:, g % 2, x // maps, kt], E[:, kt % 2, x, :w],
                                               start=(kt == 0), stop=(kt == QT - 1), tile_position=(0, 32 * x), skip_group_check=True)
                    ins.then_inc(s_pv, 1)

                def turn_results(at, g, early):
                    pe.wait_ge(s_oT, of(at, 1, g, 1))
                    if not early:
                        pe.wait_ge(s_st, of(at, 1, g, 0))
                    for j in range(QT):
                        ins = nc.tensor.transpose(pT[:, j * P:(j + 1) * P], oT[:, g % 2, j * P:(j + 1) * P], R.ident[:, :])
                    ins.then_inc(s_tr, 1)

                def body(i, first, last):
                    at = At(pe, i)
                    if first:
                        for r in range(IT):
                            pass1(at, 0, r, True)
                        turn_maxima(at, 0, True)
                        for r in range(IT):
                            pass1(at, 1, r, False)
                        pass2(at, 0, 0, True)
                    for g in range(NB):
                        for s in range(IT):
                            if not (last and g + 2 >= NB):
                                pass1(at, g + 2, s, False)
                            if s == 1 and not (last and g + 1 >= NB):
                                turn_maxima(at, g + 1, False)
                            h = g + (s + 1) // IT
                            if not (last and h >= NB):
                                pass2(at, h, (s + 1) % IT, first and h == 0)
                            if s % UN == 0 and s:
                                weigh(at, g, s // UN - 1, first and g < 2)
                            if s == 0 and not (first and g == 0):
                                weigh(at, g - 1, QT - 1, False)
                            if s == 5 and not (first and g == 0):
                                turn_results(at, g - 1, first and g == 1)
                    if last:
                        weigh(at, NB - 1, QT - 1, False)
                        turn_results(at, NB - 1, False)

                run_bodies(pe, COUNT, body)

            @block.scalar
            def _(act):
                def expo(at, g, s, first):
                    kt, x = divmod(s, UN)
                    if s == 0:
                        act.wait_ge(s_vs, of(at, 1, g, 1))
                    act.wait_ge(s_p2, of(at, IT, g, s + 1))
                    if x == 0 and not (first and g == 0 and kt < 2):
                        act.wait_ge(s_pv, of(at, QT, g, kt - 1))
                    w = T - q0(kt)
                    nc.scalar.activation(E[:, kt % 2, x, :w], pX[:, s % 2, :w], ACT.Exp, scale=gs[:, g % 2, x // maps:x // maps + 1]).then_inc(s_e, 1)

                def results(at, g, early):
                    act.wait_ge(s_pv, of(at, QT, g, QT))
                    if not early:
                        act.wait_ge(s_tr, of(at, 1, g, -1))
                    nc.scalar.activation(oT[:, g % 2], pO[:, g % 2], ACT.Copy).then_inc(s_oT, 1)

                def body(i, first, last):
                    at = At(act, i)
                    for g in range(NB):
                        for s in range(IT):
                            expo(at, g, s, first)
                            if s == 2 and not (first and g == 0):
                                results(at, g - 1, first and g < 3)
                    if last:
                        results(at, NB - 1, False)

                run_bodies(act, COUNT, body)

            @block.vector
            def _(dve):
                V = nc.vector
                V.memset(pO[:, :, :], 0.0).then_inc(s_z, 1)
                dve.wait_ge(s_c, 48 if causal else 32)
                if causal:
                    V.tensor_copy(mb[:, :, :], mk[:, :, :])
                V.tensor_copy(exb[:, :, :], ex[:, :, :]).then_inc(s_cb, 1)

                def extreme(at, h, r):
                    dve.wait_ge(s_p1, of(at, IT, h, r + 1))
                    V.reduce_max(mx[:, h % NB, r:r + 1], pS[:, r % 2, :w1(r % QT)], AX.X).then_inc(s_mx, 1)

                def split(at, i, h, early, k):
                    dve.drain()
                    if k == 0:
                        if negmax is not None:
                            V.tensor_scalar(negmax[:, bass.ds((i * NB + h) * IT, IT)], mx[:, h % NB], -DH ** -0.5, None, ALU.mult)
                        dve.wait_ge(s_mt, of(at, 1, h, 1))
                        V.tensor_scalar(m0[:, 0], pM[:IT, :P], -1.0, None, ALU.mult)
                    elif k % 2:
                        if k == 1 and not early:
                            dve.wait_ge(s_mr[(h - 2) % NB], at(48, 48 * ((h - 2) // NB + 1)))
                        ins = V.tensor_copy(mp[:, h % 2, k // 2], m0[:, k // 2])
                        if k == 5:
                            ins.then_inc(s_mp, 1)
                    else:
                        V.tensor_tensor(m0[:, k // 2], m0[:, k // 2 - 1], mp[:, h % 2, k // 2 - 1], ALU.subtract)

                def store(at, i, g, k):
                    res = pT[:, :].rearrange("p (j x d) -> p x j d", j=QT, x=UN)
                    inv = rz[:, :, :].rearrange("p j (x o) -> p x j o", o=1)
                    dst = heads[:, bass.ds((i * NB + g) * GH * QT, GH * QT), :].rearrange("p (x j) d -> p x j d", j=QT)
                    shape = [P, GH, QT, DH]
                    dve.drain()
                    if k == 0:
                        dve.wait_ge(s_tr, of(at, 1, g, 1))
                        V.reciprocal(rz[:, :, :].rearrange("p j x -> p x j"), res[:, :, :, DH])
                    elif k == 1 and maps == 1:
                        V.tensor_tensor(dst, res[:, :, :, :DH], inv.broadcast_to(shape), ALU.mult).then_inc(s_st, 1)
                    elif k == 1:
                        for x in range(GH):
                            V.scalar_tensor_tensor(out=o1[:, x], in0=res[:, 2 * x + 1, :, :DH], scalar=lamb[:, 0:1],
                                                   in1=inv[:, 2 * x + 1].broadcast_to(shape[:1] + shape[2:]), op0=ALU.mult, op1=ALU.mult)
                        V.tensor_tensor(dst, res[:, 0::2, :, :DH], inv[:, 0::2].broadcast_to(shape), ALU.mult)
                    elif maps == 2:
                        V.tensor_tensor(dst, dst, o1[:, :, :, :], ALU.add).then_inc(s_st, 1)

                def body(i, first, last):
                    at = At(dve, i)
                    if first:
                        for r in range(IT):
                            extreme(at, 0, r)
                        for k in range(6):
                            split(at, i, 0, True, k)
                        for r in range(IT):
                            extreme(at, 1, r)
                    for g in range(NB):
                        for s in range(IT):
                            if not (last and g + 2 >= NB):
                                extreme(at, g + 2, s)
                            if 2 <= s < 8 and not (last and g + 1 >= NB):
                                split(at, i, g + 1, first and g + 1 < 2, s - 2)
                            if 9 <= s < 12 and not (first and g == 0):
                                store(at, i, g - 1, s - 9)
                    if last:
                        for k in range(3):
                            store(at, i, NB - 1, k)

                run_bodies(dve, COUNT, body)


def outproj_phase(nc, R, name, heads, wo, bo=None, ln=None, mask=None):
    with phase(nc, name) as p:
        hb = p.sb("hb", [P, 2, QT, NH * DH])
        hT = p.sb("hT", [P, 2, T])
        w = p.sb("w", [P, D])
        bt = p.sb("bt", [P, QT, D])
        lw = p.sb("lw", [P, 2, QT, NH * DH])
        eps = p.sb("eps", [P, 1])
        mu = p.sb("mu", [P, 2, QT * NH])
        var = p.sb("var", [P, 2, QT * NH])
        rs = p.sb("rs", [P, 2, QT * NH])
        sq = p.sb("sq", [P, 2, QT, NH * DH])
        pT = p.ps("pT", [P, 2, T])
        pY = p.ps("pY", [P, 2, QT, D])
        s_w, s_eps, s_var, s_rs = p.sem("w"), p.sem("eps"), p.sem("var"), p.sem("rs")
        s_h = p.sem("h")
        s_t = p.sem("t")
        s_hT = p.sem("hT")
        s_y = p.sem("y")
        s_out = p.sem("out")
        NW = 1 + (bo is not None) + 2 * (ln is not None)
        NBODY = B // 2
        grp = lambda a: a.rearrange("p q (h d) -> p (q h) d", d=DH)
        wide = lambda a: a.rearrange("p (g o) -> p g o", o=1).broadcast_to([P, QT * NH, DH])
        with nc.Block() as block:
            @block.sync
            def _(sp):
                sp.dma_start(w[:, :], wo).then_inc(s_w, 16)
                if bo is not None:
                    sp.dma_start(bt[:, :, :], bo).then_inc(s_w, 16)
                if ln is not None:
                    sp.dma_start(lw[:, 0], ln[0]).then_inc(s_w, 16)
                    sp.dma_start(lw[:, 1], ln[1]).then_inc(s_w, 16)

            @block.vector
            def _(dve):
                if ln is not None:
                    nc.vector.memset(eps[:, :], EPS).then_inc(s_eps, 1)
                dve.wait_ge(s_w, 16 * NW)

                def body(i, first, last):
                    at = At(dve, i)
                    for u in range(2):
                        n = i * 2 + u
                        h = hb[:, u]
                        dve.drain()
                        if not first:
                            dve.wait_ge(s_t, at(2, u - 1))
                        src = heads[:, bass.ds(n * NH * QT, NH * QT), :]
                        if ln is not None:
                            src = src.rearrange("p (h q) d -> p q h d", q=QT)
                            nc.vector.tensor_copy(h.rearrange("p q (h d) -> p q h d", d=DH), src)
                            dve.drain()
                            nc.vector.reduce_sum(mu[:, u], grp(h), AX.X)
                            dve.drain()
                            nc.vector.tensor_scalar(mu[:, u], mu[:, u], 1.0 / DH, None, ALU.mult)
                            dve.drain()
                            nc.vector.tensor_tensor(grp(h), grp(h), wide(mu[:, u]), ALU.subtract)
                            dve.drain()
                            nc.vector.tensor_tensor(sq[:, u], h, h, ALU.mult)
                            dve.drain()
                            nc.vector.reduce_sum(var[:, u], grp(sq[:, u]), AX.X)
                            dve.drain()
                            nc.vector.tensor_scalar(var[:, u], var[:, u], 1.0 / DH, None, ALU.mult).then_inc(s_var, 1)
                            dve.wait_ge(s_rs, at(2, u + 1))
                            nc.vector.reciprocal(rs[:, u], rs[:, u])
                            dve.drain()
                            nc.vector.tensor_tensor(grp(h), grp(h), wide(rs[:, u]), ALU.mult)
                            dve.drain()
                            nc.vector.tensor_tensor(h, h, lw[:, 0], ALU.mult)
                            dve.drain()
                            nc.vector.tensor_tensor(h, h, lw[:, 1], ALU.add).then_inc(s_h, 1)
                        else:
                            for q in range(QT):
                                m = mask[:, q, bass.ds(n * NH, NH)].rearrange("p (h o) -> p h o", o=1).broadcast_to([P, NH, DH])
                                s4 = src.rearrange("p (h q) d -> p h q d", q=QT)[:, :, q, :]
                                ins = nc.vector.tensor_tensor(h[:, q].rearrange("p (h d) -> p h d", d=DH), s4, m, ALU.mult)
                            ins.then_inc(s_h, 1)
                    for u in range(2):
                        n = i * 2 + u
                        dve.wait_ge(s_y, at(2, u + 1))
                        dst = R.s[:, bass.ds(n * QT, QT), :]
                        if bo is not None:
                            nc.vector.tensor_tensor(dst, pY[:, u], bt[:, :, :], ALU.add).then_inc(s_out, 1)
                        else:
                            dve.nop(nofuse=True)
                            nc.vector.tensor_copy(dst, pY[:, u]).then_inc(s_out, 1)

                run_bodies(dve, NBODY, body)

            @block.scalar
            def _(act):
                if ln is not None:
                    act.wait_ge(s_eps, 1)

                def body(i, first, last):
                    at = At(act, i)
                    for u in range(2):
                        if ln is not None:
                            act.wait_ge(s_var, at(2, u + 1))
                            nc.scalar.activation(rs[:, u], var[:, u], ACT.Sqrt, bias=eps[:, :]).then_inc(s_rs, 1)
                        act.wait_ge(s_t, at(2, u + 1))
                        if not first:
                            act.wait_ge(s_y, at(2, u - 1))
                        nc.scalar.activation(hT[:, u], pT[:, u], ACT.Copy).then_inc(s_hT, 1)

                run_bodies(act, NBODY, body)

            @block.tensor
            def _(pe):
                pe.wait_ge(s_w, 16 * NW)

                def body(i, first, last):
                    at = At(pe, i)
                    for u in range(2):
                        pe.wait_ge(s_h, at(2, u + 1))
                        if not first:
                            pe.wait_ge(s_hT, at(2, u - 1))
                        for q in range(QT):
                            ins = nc.tensor.transpose(pT[:, u, q * P:(q + 1) * P], hb[:, u, q], R.ident[:, :])
                        ins.then_inc(s_t, 1)
                        pe.wait_ge(s_hT, at(2, u + 1))
                        if not first:
                            pe.wait_ge(s_out, at(2, u - 1))
                        for q in range(QT):
                            ins = nc.tensor.matmul(pY[:, u, q], hT[:, u, q * P:(q + 1) * P], w[:, :], start=True, stop=True)
                        ins.then_inc(s_y, 1)

                run_bodies(pe, NBODY, body)


def lambda_phase(nc, t, lam):
    with phase(nc, "lam") as p:
        l = p.sb("l", [P, 4, DH])
        pr = p.sb("pr", [P, 2, DH])
        dot = p.sb("dot", [P, 2])
        e = p.sb("e", [P, 2])
        s_in, s_dot, s_e = p.sem("in"), p.sem("dot"), p.sem("e")
        with nc.Block() as block:
            @block.sync
            def _(sp):
                for k in range(4):
                    sp.dma_start(l[:, k], t[f"l{k}"].partition_broadcast(P)).then_inc(s_in, 16)

            @block.vector
            def _(dve):
                dve.wait_ge(s_in, 64)
                nc.vector.tensor_tensor(pr[:, :, :], l[:, 0::2], l[:, 1::2], ALU.mult)
                dve.drain()
                nc.vector.reduce_sum(dot[:, :], pr[:, :, :], AX.X).then_inc(s_dot, 1)
                dve.wait_ge(s_e, 1)
                nc.vector.tensor_scalar(e[:, :], e[:, :], 0.8, None, ALU.subtract)
                dve.drain()
                nc.vector.tensor_tensor(lam[:, :], e[:, 0:1], e[:, 1:2], ALU.add)

            @block.scalar
            def _(act):
                act.wait_ge(s_dot, 1)
                nc.scalar.activation(e[:, :], dot[:, :], ACT.Exp).then_inc(s_e, 1)


def layer0_attention(nc, R, t):
    with ExitStack() as ctx:
        keep = lambda name, shape: ctx.enter_context(nc.sbuf_tensor(name, shape, F32))
        heads = keep("heads0", [P, B * NH * QT, DH])
        vtok = keep("v0", [P, B * NH, QT, DH + 1])
        lam = keep("lam", [P, 1])
        parts = nc.dram_tensor("parts0", (2, B * NH, 2, 3, DH, T), BF16).ap()
        lambda_phase(nc, t, lam)
        project_phase(nc, R, "proj0", [t[k] for k in ("wq0", "wk0", "wq1", "wk1")], t["zero4"], t["wv"], t["zero1"], parts, vtok,
                      qscale=t["qscale0"])
        attend_phase(nc, R, "att0", 2, parts, t["ext0"], t["gain0"], vtok, heads, masks=t["masks"], lamb=lam)
        outproj_phase(nc, R, "out0", heads, t["wo"], ln=(t["ln_w0"], t["ln_b0"]))


def logits_phase(nc, R, name, gw, gb, NE, lg, xT=None):
    xT = R.xnT if xT is None else xT
    with phase(nc, name) as p:
        w = p.sb("w", [P, NE])
        b = p.sb("b", [NE, 1])
        lT = p.sb("lT", [NE, 2, T])
        pl = p.ps("pl", [P, 2, T])
        pt = p.ps("pt", [P, 2, T])
        s_w, s_l, s_lT, s_t, s_lg = p.sem("w"), p.sem("l"), p.sem("lT"), p.sem("t"), p.sem("lg")
        NBODY = B // 2
        with nc.Block() as block:
            @block.sync
            def _(sp):
                sp.dma_start(w[:, :], gw).then_inc(s_w, 16)
                sp.dma_start(b[:, :], gb).then_inc(s_w, 16)

            @block.tensor
            def _(pe):
                pe.wait_ge(s_w, 32)

                def body(i, first, last):
                    at = At(pe, i)
                    for u in range(2):
                        if not first:
                            pe.wait_ge(s_lT, at(2, u - 1))
                        nc.tensor.matmul(pl[:NE, u], w[:, :], xT[:, bass.ds((i * 2 + u) * T, T)], start=True, stop=True).then_inc(s_l, 1)
                    for u in range(2):
                        pe.wait_ge(s_lT, at(2, u + 1))
                        if not first:
                            pe.wait_ge(s_lg, at(2, u - 1))
                        pe.nop(nofuse=True)
                        for q in range(QT):
                            ins = nc.tensor.transpose(pt[:, u, q * NE:(q + 1) * NE], lT[:, u, q * P:(q + 1) * P], R.ident[:NE, :NE])
                        ins.then_inc(s_t, 1)

                run_bodies(pe, NBODY, body)

            @block.scalar
            def _(act):
                act.wait_ge(s_w, 32)

                def body(i, first, last):
                    at = At(act, i)
                    for u in range(2):
                        act.wait_ge(s_l, at(2, u + 1))
                        if not first:
                            act.wait_ge(s_t, at(2, u - 1))
                        nc.scalar.activation(lT[:, u], pl[:NE, u], ACT.Identity, bias=b[:, :]).then_inc(s_lT, 1)
                    for u in range(2):
                        act.wait_ge(s_t, at(2, u + 1))
                        nc.scalar.activation(lg[:, bass.ds((i * 2 + u) * QT, QT), :],
                                             pt[:, u, :QT * NE].rearrange("p (q e) -> p q e", e=NE), ACT.Copy).then_inc(s_lg, 1)

                run_bodies(act, NBODY, body)


def top2_phase(nc, R, name, lg, NE, lower, wts, normalise, capacity=None, constants=None):
    with phase(nc, name) as p:
        mx = p.sb("mx", [P, NT, 1])
        sm = p.sb("sm", [P, NT, 1])
        pr = p.sb("pr", [P, NT, NE])
        gt = p.sb("gt", [P, NT, NE * NE])
        eq = p.sb("eq", [P, NT, NE * NE])
        lo = p.sb("lo", [P, NE * NE])
        rank = p.sb("rank", [P, NT, NE])
        s_c, s_sub, s_exp, s_sel, s_cnt = p.sem("c"), p.sem("sub"), p.sem("exp"), p.sem("sel"), p.sem("cnt")
        if capacity:
            tri = p.sb("tri", [P, 2, P])
            cnt = p.sb("cnt", [P, NT, NE])
            tot = p.sb("tot", [P, NT, NE])
            run = p.sb("run", [P, NE, NT])
            one = p.sb("one", [P, NT])
            pc = p.ps("pc", [P, 2, T])
        v3 = lambda a: a.rearrange("p t (e f) -> p t e f", e=NE)
        wide = lambda a: a.broadcast_to([P, NT, NE])
        with nc.Block() as block:
            @block.sync
            def _(sp):
                sp.dma_start(lo[:, :], lower).then_inc(s_c, 16)
                if capacity:
                    sp.dma_start(tri[:, 0], constants["upto"]).then_inc(s_c, 16)
                    sp.dma_start(tri[:, 1], constants["ones"]).then_inc(s_c, 16)

            @block.scalar
            def _(act):
                act.wait_ge(s_sub, 1)
                nc.scalar.activation(pr[:, :, :], pr[:, :, :], ACT.Exp).then_inc(s_exp, 1)

            if capacity:
                @block.tensor
                def _(pe):
                    pe.wait_ge(s_c, 48)
                    pe.wait_ge(s_sel, 1)
                    flat = rank[:, :, :].rearrange("p t e -> p (t e)")
                    nc.tensor.matmul(pc[:, 0, :NT * NE], tri[:, 0], flat, start=True, stop=True)
                    nc.tensor.matmul(pc[:, 1, :NT * NE], tri[:, 1], flat, start=True, stop=True).then_inc(s_cnt, 1)

            @block.vector
            def _(dve):
                def then(ins):
                    dve.drain()

                then(nc.vector.reduce_max(mx[:, :, 0], lg[:, :, :], AX.X))
                nc.vector.tensor_tensor(pr[:, :, :], lg[:, :, :], wide(mx[:, :, :]), ALU.subtract).then_inc(s_sub, 1)
                dve.wait_ge(s_exp, 1)
                then(nc.vector.reduce_sum(sm[:, :, 0], pr[:, :, :], AX.X))
                then(nc.vector.reciprocal(sm[:, :, :], sm[:, :, :]))
                then(nc.vector.tensor_tensor(pr[:, :, :], pr[:, :, :], wide(sm[:, :, :]), ALU.mult))
                dve.wait_ge(s_c, 48 if capacity else 16)
                for e in range(NE):
                    nc.vector.tensor_tensor(v3(gt[:, :, :])[:, :, e], pr[:, :, :], wide(pr[:, :, e:e + 1]), ALU.is_gt)
                    nc.vector.tensor_tensor(v3(eq[:, :, :])[:, :, e], pr[:, :, :], wide(pr[:, :, e:e + 1]), ALU.is_equal)
                dve.drain()
                then(nc.vector.tensor_tensor(eq[:, :, :], eq[:, :, :], lo[:, :].rearrange("p (o e) -> p o e", o=1).broadcast_to([P, NT, NE * NE]), ALU.mult))
                then(nc.vector.tensor_tensor(gt[:, :, :], gt[:, :, :], eq[:, :, :], ALU.add))
                then(nc.vector.reduce_sum(rank[:, :, :], v3(gt[:, :, :]), AX.X))
                nc.vector.tensor_scalar(rank[:, :, :], rank[:, :, :], 2.0, None, ALU.is_lt).then_inc(s_sel, 1)
                dve.drain()
                w = wts[:, :, :NE]
                then(nc.vector.tensor_tensor(w, pr[:, :, :], rank[:, :, :], ALU.mult))
                if normalise:
                    then(nc.vector.reduce_sum(sm[:, :, 0], w, AX.X))
                    then(nc.vector.reciprocal(sm[:, :, :], sm[:, :, :]))
                    then(nc.vector.tensor_tensor(w, w, wide(sm[:, :, :]), ALU.mult))
                if capacity:
                    dve.wait_ge(s_cnt, 1)
                    nc.vector.tensor_copy(cnt[:, :, :].rearrange("p t e -> p (t e)"), pc[:, 0, :NT * NE])
                    nc.vector.tensor_copy(tot[:, :, :].rearrange("p t e -> p (t e)"), pc[:, 1, :NT * NE])
                    then(nc.vector.memset(one[:, :], 1.0))
                    for e in range(NE):
                        nc.vector.tensor_tensor_scan(run[:, e], one[:, :], tot[:, :, e], 0.0, ALU.mult, ALU.add)
                    dve.drain()
                    then(nc.vector.tensor_tensor(cnt[:, :, :], cnt[:, :, :], run[:, :, :].rearrange("p e t -> p t e"), ALU.add))
                    then(nc.vector.tensor_tensor(cnt[:, :, :], cnt[:, :, :], tot[:, :, :], ALU.subtract))
                    then(nc.vector.tensor_scalar(cnt[:, :, :], cnt[:, :, :], capacity + 0.5, None, ALU.is_lt))
                    then(nc.vector.tensor_tensor(w, w, cnt[:, :, :], ALU.mult))


def turn_weights_phase(nc, R, name, wts, NE, wT, b2=None):
    with phase(nc, name) as p:
        st = p.sb("st", [P, 2, QT, NE])
        wt = p.sb("wt", [NE, 2, T])
        b = p.sb("b", [NE, D]) if b2 is not None else None
        pt = p.ps("pt", [P, 2, T])
        pf = p.ps("pf", [P, 2, T])
        s_b, s_st, s_t, s_wt, s_f, s_out = p.sem("b"), p.sem("st"), p.sem("t"), p.sem("wt"), p.sem("f"), p.sem("out")
        NBODY = B // 2
        with nc.Block() as block:
            if b2 is not None:
                @block.sync
                def _(sp):
                    sp.dma_start(b[:, :], b2).then_inc(s_b, 16)

            @block.vector
            def _(dve):
                if b2 is None:
                    nc.vector.memset(R.f[:, :, :], 0.0)

                def body(i, first, last):
                    at = At(dve, i)
                    for u in range(2):
                        n = i * 2 + u
                        if not first:
                            dve.wait_ge(s_t, at(2, u - 1))
                        dve.nop(nofuse=True)
                        nc.vector.tensor_copy(st[:, u], wts[:, bass.ds(n * QT, QT), :]).then_inc(s_st, 1)
                    for u in range(2):
                        n = i * 2 + u
                        if b2 is not None:
                            dve.wait_ge(s_f, at(2, u + 1))
                            dve.nop(nofuse=True)
                            nc.vector.tensor_copy(R.f[:, bass.ds(n * QT, QT), :].rearrange("p q d -> p (q d)"), pf[:, u]).then_inc(s_out, 1)

                run_bodies(dve, NBODY, body)

            @block.scalar
            def _(act):
                def body(i, first, last):
                    at = At(act, i)
                    for u in range(2):
                        act.wait_ge(s_t, at(2, u + 1))
                        if b2 is not None:
                            if not first:
                                act.wait_ge(s_f, at(2, u - 1))
                            nc.scalar.activation(wt[:, u], pt[:NE, u], ACT.Copy).then_inc(s_wt, 1)
                        else:
                            nc.scalar.activation(wT[:NE, bass.ds((i * 2 + u) * T, T)], pt[:NE, u], ACT.Copy).then_inc(s_wt, 1)

                run_bodies(act, NBODY, body)

            @block.tensor
            def _(pe):
                if b2 is not None:
                    pe.wait_ge(s_b, 16)

                def body(i, first, last):
                    at = At(pe, i)
                    for u in range(2):
                        pe.wait_ge(s_st, at(2, u + 1))
                        if not first:
                            pe.wait_ge(s_wt, at(2, u - 1))
                        for q in range(QT):
                            ins = nc.tensor.transpose(pt[:NE, u, q * P:(q + 1) * P], st[:, u, q], R.ident[:, :])
                        ins.then_inc(s_t, 1)
                    for u in range(2):
                        if b2 is not None:
                            pe.wait_ge(s_wt, at(2, u + 1))
                            if not first:
                                pe.wait_ge(s_out, at(2, u - 1))
                            for q in range(QT):
                                ins = nc.tensor.matmul(pf[:, u, q * P:(q + 1) * P], wt[:, u, q * P:(q + 1) * P], b[:, :], start=True, stop=True)
                            ins.then_inc(s_f, 1)

                run_bodies(pe, NBODY, body)


def experts_phase(nc, R, name, NE, w1, b1, w2, wts, U=4):
    with phase(nc, name) as p:
        a1 = p.sb("a1", [P, 2, U, P])
        a2 = p.sb("a2", [P, 2, U, D])
        bb = p.sb("bb", [P, NE, U])
        bs = p.sb("bs", [P, 2, U])
        h = p.sb("h", [P, 2, T])
        ws = p.sb("ws", [P, 2, QT, 1])
        ph = p.ps("ph", [P, 2, T])
        po = p.ps("po", [P, 2, T])
        s_b = p.sem("b")
        s_w = [p.sem("w0"), p.sem("w1")]
        s_bs = p.sem("bs")
        s_up = p.sem("up")
        s_h = p.sem("h")
        s_o = p.sem("o")
        s_f = p.sem("f")
        NBODY = NE // 2
        IT = 2 * B
        with nc.Block() as block:
            @block.sync
            def _(sp):
                sp.dma_start(bb[:, :, :], b1).then_inc(s_b, 16)

                def body(i, first, last):
                    at = At(sp, i)
                    for v in range(2):
                        e = i * 2 + v
                        if not first:
                            sp.wait_ge(s_o, at(IT, B * (v - 1)))
                        sp.dma_start(a1[:, v].rearrange("p u f -> p (u f)"), w1[bass.ds(e, 1), :, :].rearrange("o p f -> (o p) f")).then_inc(s_w[v], 16)
                        sp.dma_start(a2[:, v].rearrange("p u f -> p (u f)"), w2[bass.ds(e, 1), :, :].rearrange("o p f -> (o p) f")).then_inc(s_w[v], 16)

                run_bodies(sp, NBODY, body)

            @block.gpsimd
            def _(pool):
                pool.wait_ge(s_b, 16)

                def body(i, first, last):
                    at = At(pool, i)
                    for v in range(2):
                        if not first:
                            pool.wait_ge(s_h, at(IT * U, B * U * (v - 1)))
                        nc.gpsimd.tensor_copy(bs[:, v], bb[:, bass.ds(i * 2 + v, 1), :].rearrange("p o u -> p (o u)")).then_inc(s_bs, 1)

                run_bodies(pool, NBODY, body)

            @block.tensor
            def _(pe):
                def body(i, first, last):
                    at = At(pe, i)

                    def up(k):
                        g, u = divmod(k, U)
                        v, b = g // B % 2, g % B
                        if k % (B * U) == 0:
                            pe.wait_ge(s_w[v], at(32, 32 * (g // IT + 1)))
                        if not (first and k < 2):
                            pe.wait_ge(s_h, at(IT * U, k - 1))
                        nc.tensor.matmul(ph[:, u % 2], a1[:, v, u], R.xnT[:, b * T:(b + 1) * T], start=True, stop=True).then_inc(s_up, 1)

                    def down(g, u):
                        v, b = divmod(g, B)
                        if u == 0 and not (first and g < 2):
                            pe.wait_ge(s_f, at(IT, g - 1))
                        pe.wait_ge(s_h, at(IT * U, g * U + u + 1))
                        for q in range(QT):
                            ins = nc.tensor.matmul(po[:, g % 2, q * P:(q + 1) * P], h[:, u % 2, q * P:(q + 1) * P], a2[:, v, u],
                                                   start=(u == 0 and q == 0), stop=(u == U - 1), skip_group_check=True)
                        if u == U - 1:
                            ins.then_inc(s_o, 1)

                    if first:
                        up(0)
                    for k in range(IT * U):
                        if not (last and k + 1 >= IT * U):
                            up(k + 1)
                        down(*divmod(k, U))

                run_bodies(pe, NBODY, body)

            @block.scalar
            def _(act):
                def body(i, first, last):
                    at = At(act, i)
                    for g in range(IT):
                        v = g // B
                        if g % B == 0:
                            act.wait_ge(s_bs, at(2, v + 1))
                        for u in range(U):
                            k = g * U + u
                            act.wait_ge(s_up, at(IT * U, k + 1))
                            nc.scalar.activation(h[:, u % 2], ph[:, u % 2], ACT.Relu, bias=bs[:, v, u:u + 1]).then_inc(s_h, 1)

                run_bodies(act, NBODY, body)

            @block.vector
            def _(dve):
                def body(i, first, last):
                    at = At(dve, i)
                    for g in range(IT):
                        v, b = divmod(g, B)
                        dve.drain()
                        nc.vector.tensor_copy(ws[:, g % 2], wts[:, b * QT:(b + 1) * QT, bass.ds(i * 2 + v, 1)])
                        dve.drain()
                        dve.wait_ge(s_o, at(IT, g + 1))
                        for q in range(QT):
                            ft = R.f[:, b * QT + q]
                            ins = nc.vector.scalar_tensor_tensor(out=ft, in0=po[:, g % 2, q * P:(q + 1) * P], scalar=ws[:, g % 2, q],
                                                                 in1=ft, op0=ALU.mult, op1=ALU.add)
                        ins.then_inc(s_f, 1)

                run_bodies(dve, NBODY, body)


def layer0_gate(nc, R, t):
    with ExitStack() as ctx:
        lg = ctx.enter_context(nc.sbuf_tensor("lg0", [P, NT, 4], F32))
        wts = ctx.enter_context(nc.sbuf_tensor("wts0", [P, NT, 6], F32))
        logits_phase(nc, R, "lg_0", t["gw0"], t["gb0"], 4, lg)
        top2_phase(nc, R, "top0", lg, 4, t["lower4"], wts, False)
        with phase(nc, "half0") as p:
            with nc.Block() as block:
                @block.vector
                def _(dve):
                    nc.vector.memset(wts[:, :, 4:6], 0.5)
        turn_weights_phase(nc, R, "turn0", wts, 6, None, b2=t["b2_0"])
        experts_phase(nc, R, "ex0", 6, t["w1_0"], t["b1_0"], t["w2_0"], wts)


def pick_phase(nc, R, name, negmax, total, count, mask):
    with phase(nc, name) as p:
        N = B * NH
        GONE = -3.0e38
        sp_ = p.sb("sp", [P, QT, N])
        sT = p.sb("sT", [P, T])
        m8 = p.sb("m8", [P, 8])
        mk = p.sb("mk", [P, T])
        pT = p.ps("pT", [P, T])
        pM = p.ps("pM", [P, T])
        s_sp, s_t, s_mk, s_m = p.sem("sp"), p.sem("t"), p.sem("mk"), p.sem("m")
        scale = DH ** -0.5
        with nc.Block() as block:
            @block.vector
            def _(dve):
                for q in range(QT):
                    ins = nc.vector.scalar_tensor_tensor(
                        out=sp_[:, q].rearrange("p (b h) -> p b h", h=NH),
                        in0=total[:, :, :].rearrange("p (b q) h -> p b q h", q=QT)[:, :, q],
                        scalar=-scale / T, in1=negmax[:, :].rearrange("p (b h q) -> p b h q", h=NH, q=QT)[:, :, :, q],
                        op0=ALU.mult, op1=ALU.subtract)
                ins.then_inc(s_sp, 1)
                dve.wait_ge(s_t, 1)
                nc.vector.tensor_copy(sT[:, :], pT[:, :])
                dve.drain()
                full, more = divmod(count, 8)
                for k in range(full + (more > 0)):
                    nc.vector.max(m8[:, :], sT[:, :])
                    dve.drain()
                    if k == full:
                        nc.vector.memset(m8[:, more:], GONE)
                        dve.drain()
                    nc.vector.match_replace(sT[:, :], m8[:, :], sT[:, :], GONE)
                    dve.drain()
                nc.vector.tensor_scalar(mk[:, :], sT[:, :], GONE, None, ALU.is_equal).then_inc(s_mk, 1)
                dve.wait_ge(s_m, 1)
                nc.vector.tensor_copy(mask[:, :, :].rearrange("p q n -> p (q n)"), pM[:, :])

            @block.tensor
            def _(pe):
                pe.wait_ge(s_sp, 1)
                for q in range(QT):
                    ins = nc.tensor.transpose(pT[:, q * P:(q + 1) * P], sp_[:, q], R.ident[:, :])
                ins.then_inc(s_t, 1)
                pe.wait_ge(s_mk, 1)
                for q in range(QT):
                    ins = nc.tensor.transpose(pM[:, q * P:(q + 1) * P], mk[:, q * P:(q + 1) * P], R.ident[:, :])
                ins.then_inc(s_m, 1)


def layer1_attention(nc, R, t):
    with ExitStack() as ctx:
        keep = lambda name, shape: ctx.enter_context(nc.sbuf_tensor(name, shape, F32))
        heads = keep("heads1", [P, B * NH * QT, DH])
        vtok = keep("v1", [P, B * NH, QT, DH + 1])
        negmax = keep("negmax", [P, B * NH * QT])
        total = keep("total", [P, B * QT, NH])
        mask = keep("mask1", [P, QT, B * NH])
        parts = nc.dram_tensor("parts1", (2, B * NH, 1, 3, DH, T), BF16).ap()
        project_phase(nc, R, "proj1", [t["Wq1"], t["Wk1"]], t["bqk1"], t["Wv1"], t["bv1"], parts, vtok,
                      mean={"hmask": t["hmask"], "sum": total})
        attend_phase(nc, R, "att1", 1, parts, t["ext1"], t["gain1"], vtok, heads, negmax=negmax)
        pick_phase(nc, R, "pick", negmax, total, int(0.6 * 256), mask)
        outproj_phase(nc, R, "out1", heads, t["Wo1"], bo=t["bo1"], mask=mask)


def route_phase(nc, R, name, lg, cbias, comb):
    NE, G, M = 64, 8, 8
    CH = 8
    with phase(nc, name) as p:
        sc = p.sb("sc", [P, NT, NE])
        cb = p.sb("cb", [P, NE])
        sf = p.sb("sf", [P, CH, NE])
        hi1 = p.sb("hi1", [P, CH * G, 4])
        lo1 = p.sb("lo1", [P, CH * G, 4])
        hi2 = p.sb("hi2", [P, CH * G, 2])
        lo2 = p.sb("lo2", [P, CH * G, 2])
        t2 = p.sb("t2", [P, CH * G, 2])
        gs = p.sb("gs", [P, CH, G])
        gl = p.sb("gl", [P, CH * G, 1])
        gt = p.sb("gt", [P, CH, G * G])
        eq = p.sb("eq", [P, CH, G * G])
        lo = p.sb("lo", [P, G * G])
        gm = p.sb("gm", [P, CH, G])
        ms = p.sb("ms", [P, CH, NE])
        m8 = p.sb("m8", [P, CH, 8])
        sm = p.sb("sm", [P, CH, 1])
        s_in, s_sg = p.sem("in"), p.sem("sg")
        GONE = -3.0e38
        with nc.Block() as block:
            @block.sync
            def _(sp):
                sp.dma_start(cb[:, :], cbias[0]).then_inc(s_in, 16)
                sp.dma_start(lo[:, :], cbias[1]).then_inc(s_in, 16)

            @block.scalar
            def _(act):
                nc.scalar.activation(sc[:, :, :], lg[:, :, :], ACT.Sigmoid).then_inc(s_sg, 1)

            @block.vector
            def _(dve):
                def then(ins):
                    dve.drain()

                dve.wait_ge(s_in, 32)
                dve.wait_ge(s_sg, 1)
                with dve.Fori(0, NT // CH) as i:
                    scb = sc[:, bass.ds(i * CH, CH), :]
                    g8 = sf[:, :, :].rearrange("p t (g e) -> p (t g) e", e=8)
                    then(nc.vector.tensor_tensor(sf[:, :, :], scb, cb[:, :].rearrange("p (o e) -> p o e", o=1).broadcast_to([P, CH, NE]), ALU.add))
                    nc.vector.tensor_tensor(hi1[:, :, :], g8[:, :, 0:4], g8[:, :, 4:8], ALU.max)
                    then(nc.vector.tensor_tensor(lo1[:, :, :], g8[:, :, 0:4], g8[:, :, 4:8], ALU.min))
                    nc.vector.tensor_tensor(hi2[:, :, :], hi1[:, :, 0:2], hi1[:, :, 2:4], ALU.max)
                    nc.vector.tensor_tensor(t2[:, :, :], lo1[:, :, 0:2], lo1[:, :, 2:4], ALU.max)
                    then(nc.vector.tensor_tensor(lo2[:, :, :], hi1[:, :, 0:2], hi1[:, :, 2:4], ALU.min))
                    then(nc.vector.tensor_tensor(lo2[:, :, :], lo2[:, :, :], t2[:, :, :], ALU.max))
                    nc.vector.tensor_tensor(t2[:, :, 0:1], lo2[:, :, 0:1], lo2[:, :, 1:2], ALU.max)
                    then(nc.vector.tensor_tensor(gl[:, :, :], hi2[:, :, 0:1], hi2[:, :, 1:2], ALU.min))
                    gsf = gs[:, :, :].rearrange("p t (g o) -> p (t g) o", o=1)
                    nc.vector.tensor_tensor(gsf, hi2[:, :, 0:1], hi2[:, :, 1:2], ALU.max)
                    then(nc.vector.tensor_tensor(gl[:, :, :], gl[:, :, :], t2[:, :, 0:1], ALU.max))
                    then(nc.vector.tensor_tensor(gsf, gsf, gl[:, :, :], ALU.add))
                    v3 = lambda a: a.rearrange("p t (e f) -> p t e f", e=G)
                    for e in range(G):
                        w = gs[:, :, e:e + 1].broadcast_to([P, CH, G])
                        nc.vector.tensor_tensor(v3(gt[:, :, :])[:, :, e], gs[:, :, :], w, ALU.is_gt)
                        nc.vector.tensor_tensor(v3(eq[:, :, :])[:, :, e], gs[:, :, :], w, ALU.is_equal)
                    dve.drain()
                    then(nc.vector.tensor_tensor(eq[:, :, :], eq[:, :, :], lo[:, :].rearrange("p (o e) -> p o e", o=1).broadcast_to([P, CH, G * G]), ALU.mult))
                    then(nc.vector.tensor_tensor(gt[:, :, :], gt[:, :, :], eq[:, :, :], ALU.add))
                    then(nc.vector.reduce_sum(gm[:, :, :], v3(gt[:, :, :]), AX.X))
                    then(nc.vector.tensor_scalar(gm[:, :, :], gm[:, :, :], 4.0, None, ALU.is_lt))
                    gmw = gm[:, :, :].rearrange("p t (g o) -> p (t g) o", o=1).broadcast_to([P, CH * G, 8])
                    msg = ms[:, :, :].rearrange("p t (g e) -> p (t g) e", e=8)
                    then(nc.vector.tensor_tensor(msg, g8, gmw, ALU.mult))
                    for k in range(CH):
                        nc.vector.max(m8[:, k], ms[:, k])
                    dve.drain()
                    for k in range(CH):
                        nc.vector.match_replace(sf[:, k], m8[:, k], ms[:, k], GONE)
                    dve.drain()
                    then(nc.vector.tensor_scalar(sf[:, :, :], sf[:, :, :], GONE, None, ALU.is_equal))
                    cm = comb[:, bass.ds(i * CH, CH), 0:NE]
                    then(nc.vector.tensor_tensor(ms[:, :, :], sf[:, :, :], scb, ALU.mult))
                    then(nc.vector.reduce_sum(sm[:, :, 0], ms[:, :, :], AX.X))
                    then(nc.vector.tensor_scalar(sm[:, :, :], sm[:, :, :], 1e-20, None, ALU.add))
                    then(nc.vector.reciprocal(sm[:, :, :], sm[:, :, :]))
                    then(nc.vector.tensor_tensor(ms[:, :, :], ms[:, :, :], sm[:, :, :].broadcast_to([P, CH, NE]), ALU.mult))
                    then(nc.vector.tensor_scalar(cm, ms[:, :, :], 2.5, None, ALU.mult))


def pairs_phase(nc, R, name, NPAIR, w1, w2, sel, cA, cB):
    NC = cB.shape[0]
    with phase(nc, name) as p:
        a = p.sb("a", [P, 2, 4, P])
        sb_ = p.sb("sb", [P, 2, 2, P], BF16)
        r = p.sb("r", [P, 2, T])
        c = p.sb("c", [P, 2, T])
        h = p.sb("h", [P, 2, T])
        ph = p.ps("ph", [P, 2, T])
        pc = p.ps("pc", [P, 2, T])
        po = p.ps("po", [P, 2, T])
        s_w = [p.sem("w0"), p.sem("w1")]
        s_sel = p.sem("sel")
        s_up = p.sem("up")
        s_r = p.sem("r")
        s_c = p.sem("c")
        s_h = p.sem("h")
        s_o = p.sem("o")
        s_f = p.sem("f")
        NBODY = NPAIR // 2
        IT = 2 * B
        with nc.Block() as block:
            @block.sync
            def _(sp):
                def body(i, first, last):
                    at = At(sp, i)
                    for v in range(2):
                        e = i * 2 + v
                        if not first:
                            sp.wait_ge(s_o, at(IT, B * (v - 1)))
                        for k, src in enumerate((w1, w2, sel)):
                            dst = a[:, v, k] if k < 2 else a[:, v, 2:].rearrange("p k f -> p (k f)")
                            sp.dma_start(dst, src[bass.ds(e, 1), :, :].rearrange("o p f -> (o p) f")).then_inc(s_w[v], 16)

                run_bodies(sp, NBODY, body)

            @block.gpsimd
            def _(pool):
                def body(i, first, last):
                    at = At(pool, i)

                    def convert(e):
                        pool.wait_ge(s_w[e % 2], at(48, 48 * (e // 2 + 1)))
                        pool.nop(nofuse=True)
                        nc.gpsimd.tensor_copy(sb_[:, e % 2], a[:, e % 2, 2:]).then_inc(s_sel, 1)

                    if first:
                        convert(0)
                    for g in range(IT):
                        if g == 2:
                            convert(1)
                        if g == B + 2 and not last:
                            convert(2)
                        pool.wait_ge(s_c, at(IT, g + 1))
                        if not (first and g < 2):
                            pool.wait_ge(s_o, at(IT, g - 1))
                        nc.gpsimd.tensor_tensor(h[:, g % 2], c[:, g % 2], r[:, g % 2], ALU.mult).then_inc(s_h, 1)

                run_bodies(pool, NBODY, body)

            @block.tensor
            def _(pe):
                def body(i, first, last):
                    at = At(pe, i)

                    def up(g, first):
                        v, b = (g // B) % 2, g % B
                        if g % B == 0:
                            pe.wait_ge(s_w[v], at(48, 48 * (g // IT + 1)))
                            pe.wait_ge(s_sel, at(2, g // B + 1))
                        if not (first and g < 2):
                            pe.wait_ge(s_c, at(IT, g - 1))
                        nc.tensor.matmul(ph[:, g % 2], a[:, v, 0], R.xnT[:, b * T:(b + 1) * T], start=True, stop=True)
                        nc.tensor.matmul(pc[:, g % 2], sb_[:, v, 0], cA[:, b * T:(b + 1) * T], start=True, stop=False)
                        nc.tensor.matmul(pc[:, g % 2], sb_[:NC, v, 1], cB[:, b * T:(b + 1) * T], start=False, stop=True).then_inc(s_up, 1)

                    def down(g, first):
                        v = g // B
                        pe.wait_ge(s_h, at(IT, g + 1))
                        if not (first and g < 2):
                            pe.wait_ge(s_f, at(IT, g - 1))
                        for q in range(QT):
                            ins = nc.tensor.matmul(po[:, g % 2, q * P:(q + 1) * P], h[:, g % 2, q * P:(q + 1) * P], a[:, v, 1], start=True, stop=True)
                        ins.then_inc(s_o, 1)

                    if first:
                        up(0, True)
                        up(1, True)
                    for g in range(IT):
                        if not (last and g + 2 >= IT):
                            up(g + 2, first)
                        down(g, first)

                run_bodies(pe, NBODY, body)

            @block.scalar
            def _(act):
                def body(i, first, last):
                    at = At(act, i)
                    for g in range(IT):
                        act.wait_ge(s_up, at(IT, g + 1))
                        if not (first and g < 2):
                            act.wait_ge(s_h, at(IT, g - 1))
                        nc.scalar.activation(r[:, g % 2], ph[:, g % 2], ACT.Relu).then_inc(s_r, 1)

                run_bodies(act, NBODY, body)

            @block.vector
            def _(dve):
                def body(i, first, last):
                    at = At(dve, i)

                    def hidden(g, first):
                        dve.wait_ge(s_r, at(IT, g + 1))
                        if not (first and g < 2):
                            dve.wait_ge(s_h, at(IT, g - 1))
                        nc.vector.tensor_tensor(c[:, g % 2], pc[:, g % 2], r[:, g % 2], ALU.mult).then_inc(s_c, 1)

                    def add(g):
                        b = g % B
                        f = R.f[:, b * QT:(b + 1) * QT, :].rearrange("p q d -> p (q d)")
                        dve.wait_ge(s_o, at(IT, g + 1))
                        nc.vector.tensor_tensor(f, po[:, g % 2], f, ALU.add).then_inc(s_f, 1)

                    if first:
                        hidden(0, True)
                        hidden(1, True)
                    for g in range(IT):
                        if not (last and g + 2 >= IT):
                            hidden(g + 2, first)
                        add(g)

                run_bodies(dve, NBODY, body)


def layer1_gate(nc, R, t):
    with ExitStack() as ctx:
        keep = lambda name, shape: ctx.enter_context(nc.sbuf_tensor(name, shape, F32))
        lg = keep("lg1", [P, NT, 64])
        comb = keep("comb", [P, NT, 64])
        cmbA = keep("cmbA", [P, NT, P])
        cmbB = keep("cmbB", [P, NT, 65])
        cA = ctx.enter_context(nc.sbuf_tensor("cA", [P, B * T], BF16))
        cB = ctx.enter_context(nc.sbuf_tensor("cB", [65, B * T], BF16))
        part = ctx.enter_context(nc.sbuf_tensor("cpart", [P, NT, 64], BF16))
        logits_phase(nc, R, "lg_1", t["rw1"], t["rb1"], 64, lg)
        route_phase(nc, R, "route", lg, (t["cbias"], t["lower8"]), comb)
        with phase(nc, "one1") as p:
            with nc.Block() as block:
                @block.vector
                def _(dve):
                    c, r = comb[:, :, :], cmbB[:, :, :64]
                    nc.vector.memset(cmbB[:, :, 64:], 1.0)
                    nc.vector.tensor_copy(part[:, :, :], c)
                    dve.drain()
                    nc.vector.tensor_copy(cmbA[:, :, :64], part[:, :, :])
                    nc.vector.tensor_tensor(r, c, part[:, :, :], ALU.subtract)
                    dve.drain()
                    nc.vector.tensor_copy(part[:, :, :], r)
                    dve.drain()
                    nc.vector.tensor_copy(cmbA[:, :, 64:], part[:, :, :])
                    nc.vector.tensor_tensor(r, r, part[:, :, :], ALU.subtract)
        turn_weights_phase(nc, R, "turn1a", cmbA, P, cA)
        turn_weights_phase(nc, R, "turn1b", cmbB, 65, cB)
        pairs_phase(nc, R, "pairs", 34, t["up1"], t["down1"], t["sel1"], cA, cB)


def layer2_gate(nc, R, t):
    with ExitStack() as ctx:
        lg = ctx.enter_context(nc.sbuf_tensor("lg2", [P, NT, 8], F32))
        wts = ctx.enter_context(nc.sbuf_tensor("wts2", [P, NT, 8], F32))
        logits_phase(nc, R, "lg_2", t["gw2"], t["gb2"], 8, lg)
        top2_phase(nc, R, "top2", lg, 8, t["lower8"], wts, True, capacity=int(1.25 * B * T / 8), constants=t)
        turn_weights_phase(nc, R, "turn2", wts, 8, None, b2=t["b2_2"])
        experts_phase(nc, R, "ex2", 8, t["w1_2"], t["b1_2"], t["w2_2"], wts)


def layer3_gate(nc, R, t):
    U = 3
    with phase(nc, "glu") as p:
        wi = p.sb("wi", [P, 3, U, P], I32)
        w = p.sb("w", [P, 3, U, P])
        g = p.sb("g", [P, 2, T])
        h = p.sb("h", [P, 2, T])
        pg = p.ps("pg", [P, 2, T])
        pu = p.ps("pu", [P, 2, T])
        po = p.ps("po", [P, 2, T])
        s_in, s_w, s_up, s_g, s_h, s_d, s_o, s_f = (p.sem(k) for k in ("in", "w", "up", "g", "h", "d", "o", "f"))
        NBODY = B // 2
        IT = 2 * U
        with nc.Block() as block:
            @block.sync
            def _(sp):
                sp.dma_start(wi[:, :, :, :].rearrange("p k u f -> p (k u f)"), t["w3"]).then_inc(s_in, 16)

            @block.scalar
            def _(act):
                def body(i, first, last):
                    at = At(act, i)
                    for k in range(IT):
                        act.wait_ge(s_up, at(IT, k + 1))
                        if not (first and k < 2):
                            act.wait_ge(s_h, at(IT, k - 1))
                        nc.scalar.activation(g[:, k % 2], pg[:, k % 2], ACT.Silu).then_inc(s_g, 1)

                run_bodies(act, NBODY, body)

            @block.tensor
            def _(pe):
                pe.wait_ge(s_w, 1)

                def body(i, first, last):
                    at = At(pe, i)

                    def up(k, first):
                        v, u = divmod(k, U)
                        xb = R.xnT[:, bass.ds((i * 2 + v) * T, T)]
                        if not (first and k < 2):
                            pe.wait_ge(s_h, at(IT, k - 1))
                        nc.tensor.matmul(pg[:, k % 2], w[:, 0, u], xb, start=True, stop=True)
                        nc.tensor.matmul(pu[:, k % 2], w[:, 1, u], xb, start=True, stop=True).then_inc(s_up, 1)

                    def down(k, first):
                        v, u = divmod(k, U)
                        if u == 0 and not first:
                            pe.wait_ge(s_f, at(2, v - 1))
                        pe.wait_ge(s_h, at(IT, k + 1))
                        for q in range(QT):
                            ins = nc.tensor.matmul(po[:, v, q * P:(q + 1) * P], h[:, k % 2, q * P:(q + 1) * P], w[:, 2, u],
                                                   start=(u == 0 and q == 0), stop=(u == U - 1), skip_group_check=True)
                        ins.then_inc(s_d, 1)

                    if first:
                        up(0, True)
                    for k in range(IT):
                        if not (last and k + 1 >= IT):
                            up(k + 1, first)
                        down(k, first)

                run_bodies(pe, NBODY, body)

            @block.vector
            def _(dve):
                dve.wait_ge(s_in, 16)
                nc.vector.tensor_scalar(w[:, :, :, :].rearrange("p k u f -> p (k u f)"), wi[:, :, :, :].rearrange("p k u f -> p (k u f)"),
                                        float(np.float32(1.0 / 127.0)), None, ALU.mult).then_inc(s_w, 1)

                def body(i, first, last):
                    at = At(dve, i)

                    def hidden(k, first):
                        dve.wait_ge(s_g, at(IT, k + 1))
                        if not (first and k < 2):
                            dve.wait_ge(s_d, at(IT, k - 1))
                        nc.vector.tensor_tensor(h[:, k % 2], pu[:, k % 2], g[:, k % 2], ALU.mult).then_inc(s_h, 1)

                    if first:
                        hidden(0, True)
                    for k in range(IT):
                        if not (last and k + 1 >= IT):
                            hidden(k + 1, first)
                        v, u = divmod(k, U)
                        if u == U - 1:
                            dve.wait_ge(s_d, at(IT, k + 1))
                            dve.nop(nofuse=True)
                            nc.vector.tensor_copy(R.f[:, bass.ds((i * 2 + v) * QT, QT), :].rearrange("p q d -> p (q d)"),
                                                  po[:, v]).then_inc(s_f, 1)

                run_bodies(dve, NBODY, body)


def layer3_attention(nc, R, t):
    PAIRS, DW = 8, 64
    IR = 2 * QT
    N = B * PAIRS
    ROWS = 2 * IR
    BW = T + (QT - 1) * P
    with phase(nc, "att3") as p:
        allbias = p.sb("allbias", [P, PAIRS, 2 * BW])
        bias = p.sb("bias", [P, 2, 2 * BW])
        w = p.sb("w", [P, 2, 3, P])
        wo = p.sb("wo", [P, 2, P])
        xb = p.sb("xb", [P, 2, T])
        q2 = p.sb("q2", [P, 2, 2, T])
        kT = p.sb("kT", [P, 2, T])
        v = p.sb("v", [P, 2, QT, P])
        S = p.sb("S", [P, 2, T])
        nm = p.sb("nm", [P, 2, IR])
        E = p.sb("E", [P, 2, T])
        Z = p.sb("Z", [P, 2, IR])
        rz = p.sb("rz", [P, 2, IR])
        WT = p.sb("WT", [P, 2, T])
        o = p.sb("o", [P, QT, 2, DW])
        oT = p.sb("oT", [P, T])
        bo = p.sb("bo", [P, QT * D])
        pA = p.ps("pA", [P, T])
        pS = p.ps("pS", [P, 2, T])
        pT = p.ps("pT", [P, 2, T])
        pO = p.ps("pO", [P, T])
        pX = p.ps("pX", [P, T])
        pY = p.ps("pY", [P, T])
        s_c = p.sem("c")
        s_z = p.sem("z")
        s_w = [p.sem("w0"), p.sem("w1")]
        s_wo = [p.sem("wo0"), p.sem("wo1")]
        s_b = p.sem("b")
        s_pr = p.sem("pr")
        s_pc = p.sem("pc")
        s_sc = p.sem("sc")
        s_mx = p.sem("mx")
        s_e = p.sem("e")
        s_t = p.sem("t")
        s_wt = p.sem("wt")
        s_o = p.sem("o")
        s_on = p.sem("on")
        s_ot = p.sem("ot")
        s_oc = p.sem("oc")
        s_y = p.sem("y")
        s_add = p.sem("add")
        width = lambda j: (j + 1) * P
        COUNT = N // 2
        split = lambda r: (r // IR % 2, r % IR // QT, r % QT)
        with nc.Block() as block:
            @block.sync
            def _(sp):
                sp.dma_start(allbias[:, :, :], t["bias3"]).then_inc(s_c, 16)
                sp.dma_start(bo[:, :], t["bo3"]).then_inc(s_c, 16)

                def body(i, first, last):
                    at = At(sp, i)
                    for u in range(2):
                        a, b = i % 4 * 2 + u, i // 4
                        if not first:
                            sp.wait_ge(s_pr, at(6, 3 * (u - 1)))
                        sp.dma_start(w[:, u].rearrange("p k f -> p (k f)"), t["w3a"][bass.ds(a, 1), :, :].rearrange("o p f -> (o p) f")).then_inc(s_w[u], 16)
                        sp.dma_start(xb[:, u], R.xnT[:, bass.ds(b * T, T)]).then_inc(s_w[u], 16)
                        if not first:
                            sp.wait_ge(s_y, at(2, u - 1))
                        sp.dma_start(wo[:, u], t["wo3"][bass.ds(a, 1), :, :].rearrange("o p f -> (o p) f")).then_inc(s_wo[u], 16)

                run_bodies(sp, COUNT, body)

            @block.gpsimd
            def _(pool):
                nc.gpsimd.memset(q2[:, :, :, :], 0.0).then_inc(s_z, 1)
                pool.wait_ge(s_c, 32)

                def body(i, first, last):
                    at = At(pool, i)
                    for u in range(2):
                        if not first:
                            pool.wait_ge(s_mx, at(ROWS, IR * (u - 1)))
                        nc.gpsimd.tensor_copy(bias[:, u], allbias[:, bass.ds(i % 4 * 2 + u, 1), :].rearrange("p o f -> p (o f)")).then_inc(s_b, 1)

                run_bodies(pool, COUNT, body)

            @block.tensor
            def _(pe):
                def project(at, k, m):
                    u = m % 2
                    if k == 0:
                        pe.wait_ge(s_w[u], at(32, 32 * (m // 2 + 1)))
                    if not (isinstance(at.i, int) and at.i == 0 and m == 0 and k == 0):
                        pe.wait_ge(s_pc, at(6, 3 * m + k))
                    if k < 2:
                        ins = nc.tensor.matmul(pA[:, :], w[:, u, k], xb[:, u], start=True, stop=True)
                    else:
                        for q in range(QT):
                            ins = nc.tensor.matmul(pA[:, q * P:(q + 1) * P], xb[:, u, q * P:(q + 1) * P], w[:, u, 2], start=True, stop=True)
                    ins.then_inc(s_pr, 1)

                def scores(at, r, first):
                    u, h, j = split(r)
                    if r % IR == 0:
                        pe.wait_ge(s_pc, at(6, 3 * (r // IR) + 2))
                    if not (first and r < 2):
                        pe.wait_ge(s_mx, at(ROWS, r - 1))
                    nc.tensor.matmul(pS[:, r % 2, :width(j)], q2[:, u, h, j * P:(j + 1) * P], kT[:, u, :width(j)],
                                     start=True, stop=True).then_inc(s_sc, 1)

                def turn(at, r, first):
                    j = r % QT
                    pe.wait_ge(s_e, at(ROWS, r + 1))
                    if not (first and r < 2):
                        pe.wait_ge(s_wt, at(ROWS, r - 1))
                    for k in range(j + 1):
                        ins = nc.tensor.transpose(pT[:, r % 2, k * P:(k + 1) * P], E[:, r % 2, k * P:(k + 1) * P], R.ident[:, :])
                    ins.then_inc(s_t, 1)

                def weigh(at, r, first):
                    u, h, j = split(r)
                    if r % IR == 0:
                        pe.wait_ge(s_pc, at(6, 3 * (r // IR) + 3))
                        if not (first and r == 0):
                            pe.wait_ge(s_on, at(2, r // IR))
                    pe.wait_ge(s_wt, at(ROWS, r + 1))
                    dst = pO[:, (h * QT + j) * DW:(h * QT + j + 1) * DW]
                    for k in range(j + 1):
                        ins = nc.tensor.matmul(dst, WT[:, r % 2, k * P:(k + 1) * P], v[:, u, k, h * DW:(h + 1) * DW], start=(k == 0), stop=(k == j))
                    ins.then_inc(s_o, 1)

                def turn_outputs(at, m, first_item):
                    pe.wait_ge(s_on, at(2, m + 1))
                    if not first_item:
                        pe.wait_ge(s_oc, at(2, m))
                    for q in range(QT):
                        ins = nc.tensor.transpose(pX[:, q * P:(q + 1) * P], o[:, q].rearrange("p h d -> p (h d)"), R.ident[:, :])
                    ins.then_inc(s_ot, 1)

                def through_wo(at, m, first_item):
                    u = m % 2
                    pe.wait_ge(s_wo[u], at(16, 16 * (m // 2 + 1)))
                    pe.wait_ge(s_oc, at(2, m + 1))
                    if not first_item:
                        pe.wait_ge(s_add, at(2, m))
                    for q in range(QT):
                        ins = nc.tensor.matmul(pY[:, q * P:(q + 1) * P], oT[:, q * P:(q + 1) * P], wo[:, u], start=True, stop=True)
                    ins.then_inc(s_y, 1)

                def body(i, first, last):
                    at = At(pe, i)
                    if first:
                        pe.wait_ge(s_z, 2)
                        for k in range(3):
                            project(at, k, 0)
                        scores(at, 0, True)
                        scores(at, 1, True)
                        turn(at, 0, True)
                    for r in range(ROWS):
                        m, rr = divmod(r, IR)
                        if rr in (0, 2, 4) and not (last and m == 1):
                            project(at, rr // 2, m + 1)
                        if not (last and r + 2 >= ROWS):
                            scores(at, r + 2, first)
                        if not (last and r + 1 >= ROWS):
                            turn(at, r + 1, first)
                        weigh(at, r, first)
                        if rr == 2 and not (first and m == 0):
                            turn_outputs(at, m - 1, first and m == 1)
                        if rr == 4 and not (first and m == 0):
                            through_wo(at, m - 1, first and m == 1)
                    if last:
                        turn_outputs(at, 1, False)
                        through_wo(at, 1, False)

                run_bodies(pe, COUNT, body)

            @block.scalar
            def _(act):
                def leave(at, k, m, first_two):
                    u = m % 2
                    act.wait_ge(s_pr, at(6, 3 * m + k + 1))
                    if not first_two:
                        act.wait_ge(s_sc if k < 2 else s_o, at(ROWS, IR * (m - 1)))
                    if k == 0:
                        nc.scalar.activation(q2[0:DW, u, 0], pA[0:DW, :], ACT.Copy)
                        ins = nc.scalar.activation(q2[DW:, u, 1], pA[DW:, :], ACT.Copy)
                    elif k == 1:
                        ins = nc.scalar.activation(kT[:, u], pA[:, :], ACT.Copy)
                    else:
                        ins = nc.scalar.activation(v[:, u].rearrange("p q f -> p (q f)"), pA[:, :], ACT.Copy)
                    ins.then_inc(s_pc, 1)

                def expo(at, r, first):
                    u, h, j = split(r)
                    act.wait_ge(s_mx, at(ROWS, r + 1))
                    if not (first and r < 2):
                        act.wait_ge(s_t, at(ROWS, r - 1))
                    k = r % IR
                    nc.scalar.activation(E[:, r % 2, :width(j)], S[:, r % 2, :width(j)], ACT.Exp, bias=nm[:, u, k:k + 1], scale=-1.0,
                                         accum_out=Z[:, u, k:k + 1]).then_inc(s_e, 1)

                def copy(at, r, first):
                    j = r % QT
                    act.wait_ge(s_t, at(ROWS, r + 1))
                    if not (first and r < 2):
                        act.wait_ge(s_o, at(ROWS, r - 1))
                    nc.scalar.activation(WT[:, r % 2, :width(j)], pT[:, r % 2, :width(j)], ACT.Copy).then_inc(s_wt, 1)

                def outputs(at, m, first_item):
                    act.wait_ge(s_ot, at(2, m + 1))
                    if not first_item:
                        act.wait_ge(s_y, at(2, m))
                    nc.scalar.activation(oT[:, :], pX[:, :], ACT.Copy).then_inc(s_oc, 1)

                def body(i, first, last):
                    at = At(act, i)
                    if first:
                        act.wait_ge(s_z, 2)
                        for k in range(3):
                            leave(at, k, 0, True)
                        expo(at, 0, True)
                        expo(at, 1, True)
                        copy(at, 0, True)
                    for r in range(ROWS):
                        m, rr = divmod(r, IR)
                        if rr in (0, 2, 4) and not (last and m == 1):
                            leave(at, rr // 2, m + 1, first and m == 0)
                        if not (last and r + 2 >= ROWS):
                            expo(at, r + 2, first)
                        if not (last and r + 1 >= ROWS):
                            copy(at, r + 1, first)
                        if rr == 2 and not (first and m == 0):
                            outputs(at, m - 1, first and m == 1)
                    if last:
                        outputs(at, 1, False)

                run_bodies(act, COUNT, body)

            @block.vector
            def _(dve):
                dve.wait_ge(s_c, 32)
                nc.vector.tensor_copy(R.s[:, :, :].rearrange("p (b q) d -> p b (q d)", q=QT),
                                      bo[:, :].rearrange("p (o f) -> p o f", o=1).broadcast_to([P, B, QT * D])).then_inc(s_z, 1)

                def extreme(at, r, first):
                    u, h, j = split(r)
                    w_ = width(j)
                    dve.drain()
                    dve.wait_ge(s_sc, at(ROWS, r + 1))
                    if r % IR == 0:
                        dve.wait_ge(s_b, at(2, r // IR + 1))
                    if not (first and r < 2):
                        dve.wait_ge(s_e, at(ROWS, r - 1))
                    dve.nop(nofuse=True)
                    off = h * BW + (QT - 1 - j) * P
                    k = r % IR
                    nc.vector.tensor_tensor_reduce(out=S[:, r % 2, :w_], in0=pS[:, r % 2, :w_], in1=bias[:, u, off:off + w_], scale=-1.0 / DW,
                                                   scalar=3.0e38, op0=ALU.add, op1=ALU.min, accum_out=nm[:, u, k:k + 1]).then_inc(s_mx, 1)

                def divide(at, m, first_item):
                    u = m % 2
                    dve.wait_ge(s_o, at(ROWS, IR * (m + 1)))
                    nc.vector.reciprocal(rz[:, u], Z[:, u])
                    dve.drain()
                    if not first_item:
                        dve.wait_ge(s_ot, at(2, m))
                    for h in range(2):
                        ins = nc.vector.tensor_tensor(o[:, :, h], pO[:, h * QT * DW:(h + 1) * QT * DW].rearrange("p (q d) -> p q d", d=DW),
                                                      rz[:, u, h * QT:(h + 1) * QT].rearrange("p (q o) -> p q o", o=1).broadcast_to([P, QT, DW]), ALU.mult)
                    ins.then_inc(s_on, 1)

                def add(at, i, m):
                    b = (i * 2 + m) // PAIRS
                    dst = R.s[:, bass.ds(b * QT, QT), :].rearrange("p q d -> p (q d)")
                    dve.drain()
                    dve.wait_ge(s_y, at(2, m + 1))
                    nc.vector.tensor_tensor(dst, pY[:, :], dst, ALU.add).then_inc(s_add, 1)

                def body(i, first, last):
                    at = At(dve, i)
                    if first:
                        extreme(at, 0, True)
                        extreme(at, 1, True)
                    for r in range(ROWS):
                        m, rr = divmod(r, IR)
                        if rr == 0 and not (first and m == 0):
                            divide(at, m - 1, first and m == 1)
                        if not (last and r + 2 >= ROWS):
                            extreme(at, r + 2, first)
                        if rr == 4 and not (first and m == 0):
                            add(at, i, m - 1)
                    if last:
                        divide(at, 1, False)
                        add(at, i, 1)

                run_bodies(dve, COUNT, body)


H2, HK, HV, C = 4, 32, 64, 32
NC2 = T // C
HALF = B // 2


def decay_phase(nc, R, name, lg, ab, a_log):
    with phase(nc, name) as p:
        W4 = [P, NT, H2]
        z, az, e, s, s2, q = (p.sb(k, W4) for k in ("z", "az", "e", "s", "s2", "q"))
        al = p.sb("al", [P, H2])
        s_c, s_al, s_e, s_az, s_g = (p.sem(k) for k in ("c", "al", "e", "az", "g"))
        with nc.Block() as block:
            @block.sync
            def _(sp):
                sp.dma_start(al[:, :], a_log).then_inc(s_c, 16)

            @block.scalar
            def _(act):
                nc.scalar.activation(ab[:, :, 0], lg[:, :, :H2], ACT.Sigmoid)
                act.wait_ge(s_c, 16)
                nc.scalar.activation(al[:, :], al[:, :], ACT.Exp).then_inc(s_al, 1)
                act.wait_ge(s_az, 1)
                nc.scalar.activation(e[:, :, :], az[:, :, :], ACT.Exp, scale=-1.0).then_inc(s_e, 1)
                act.wait_ge(s_g, 1)
                nc.scalar.activation(ab[:, :, 1], q[:, :, :], ACT.Exp, scale=-1.0)

            @block.vector
            def _(dve):
                def then(ins):
                    dve.drain()

                then(nc.vector.tensor_copy(z[:, :, :], lg[:, :, H2:]))
                then(nc.vector.tensor_scalar(az[:, :, :], z[:, :, :], -1.0, None, ALU.mult))
                nc.vector.tensor_tensor(az[:, :, :], az[:, :, :], z[:, :, :], ALU.max).then_inc(s_az, 1)
                dve.wait_ge(s_e, 1)
                then(nc.vector.tensor_scalar(s[:, :, :], e[:, :, :], 2.0, None, ALU.add))
                then(nc.vector.reciprocal(s[:, :, :], s[:, :, :]))
                then(nc.vector.tensor_tensor(s[:, :, :], s[:, :, :], e[:, :, :], ALU.mult))
                then(nc.vector.tensor_tensor(s2[:, :, :], s[:, :, :], s[:, :, :], ALU.mult))
                then(nc.vector.tensor_scalar(q[:, :, :], s2[:, :, :], 1.0 / 17, None, ALU.mult))
                for k in range(15, 1, -2):
                    then(nc.vector.scalar_tensor_tensor(out=q[:, :, :], in0=q[:, :, :], scalar=1.0 / k, in1=s2[:, :, :], op0=ALU.add, op1=ALU.mult))
                then(nc.vector.scalar_tensor_tensor(out=q[:, :, :], in0=q[:, :, :], scalar=1.0, in1=s[:, :, :], op0=ALU.add, op1=ALU.mult))
                then(nc.vector.tensor_scalar(q[:, :, :], q[:, :, :], 2.0, None, ALU.mult))
                then(nc.vector.tensor_scalar(z[:, :, :], z[:, :, :], 0.0, None, ALU.max))
                then(nc.vector.tensor_tensor(q[:, :, :], q[:, :, :], z[:, :, :], ALU.add))
                dve.wait_ge(s_al, 1)
                nc.vector.tensor_tensor(q[:, :, :], q[:, :, :], al[:, :].rearrange("p (o h) -> p o h", o=1).broadcast_to(W4), ALU.mult).then_inc(s_g, 1)


def conv_phase(nc, R, name, w, taps, q, k, v):
    PAD = 3
    with phase(nc, name) as p:
        ws = p.sb("ws", [P, 4, P])
        ts = p.sb("ts", [P, 4, 4])
        raw = p.sb("raw", [P, 2, PAD + T])
        y = p.sb("y", [P, 2, T])
        vy = p.sb("vy", [P, 2, T])
        vt = p.sb("vt", [P, 2, T])
        ps = p.ps("ps", [P, 2, T])
        s_w, s_mm, s_raw, s_conv, s_silu, s_turn, s_v = (p.sem(n) for n in ("w", "mm", "raw", "conv", "silu", "turn", "v"))
        IT = 8
        with nc.Block() as block:
            @block.sync
            def _(sp):
                sp.dma_start(ws[:, :, :], w).then_inc(s_w, 16)
                sp.dma_start(ts[:, :, :], taps).then_inc(s_w, 16)

            @block.tensor
            def _(pe):
                pe.wait_ge(s_w, 32)

                def body(i, first, last):
                    at = At(pe, i)
                    for g in range(IT):
                        u, m = divmod(g, 4)
                        if not (first and g < 2):
                            pe.wait_ge(s_raw, at(IT, g - 1))
                        nc.tensor.matmul(ps[:, g % 2], ws[:, m], R.xn2T[:, bass.ds((i + u * HALF) * T, T)], start=True, stop=True).then_inc(s_mm, 1)

                run_bodies(pe, HALF, body)

            @block.scalar
            def _(act):
                def copy(at, g, first):
                    act.wait_ge(s_mm, at(IT, g + 1))
                    if not (first and g < 2):
                        act.wait_ge(s_conv, at(IT, g - 1))
                    nc.scalar.activation(raw[:, g % 2, PAD:], ps[:, g % 2], ACT.Copy).then_inc(s_raw, 1)

                def silu(at, i, g, first):
                    u, m = divmod(g, 4)
                    act.wait_ge(s_conv, at(IT, g + 1))
                    if m < 2:
                        dst = (q, k)[m][:, bass.ds((i + u * HALF) * T, T)]
                    else:
                        dst = vy[:, m % 2]
                        if not (first and u == 0):
                            act.wait_ge(s_turn, at(4, 2 * u + m - 3))
                    nc.scalar.activation(dst, y[:, g % 2], ACT.Silu).then_inc(s_silu, 1)

                def body(i, first, last):
                    at = At(act, i)
                    if first:
                        copy(at, 0, True)
                    for g in range(IT):
                        if not (last and g + 1 >= IT):
                            copy(at, g + 1, first)
                        silu(at, i, g, first)

                run_bodies(act, HALF, body)

            @block.vector
            def _(dve):
                nc.vector.memset(raw[:, :, :PAD], 0.0)
                dve.drain()
                dve.wait_ge(s_w, 32)

                def conv(at, g, first):
                    m = g % 4
                    r, o = raw[:, g % 2], y[:, g % 2]
                    dve.wait_ge(s_raw, at(IT, g + 1))
                    if not (first and g < 2):
                        dve.wait_ge(s_silu, at(IT, g - 1))
                    nc.vector.tensor_scalar(o, r[:, 0:T], ts[:, m, 0:1], None, ALU.mult)
                    for n in range(1, 4):
                        dve.drain()
                        ins = nc.vector.scalar_tensor_tensor(out=o, in0=r[:, n:n + T], scalar=ts[:, m, n:n + 1], in1=o, op0=ALU.mult, op1=ALU.add)
                    ins.then_inc(s_conv, 1)

                def turn(at, g, back, first):
                    u, m = divmod(g, 4)
                    dve.wait_ge(s_silu, at(IT, g + 1 - back * IT))
                    if not (first and u == 0):
                        dve.wait_ge(s_v, at(4, 2 * u + m - 3 - back * 4))
                    dve.nop(nofuse=True)
                    nc.vector.transpose(vt[:, m % 2], vy[:, m % 2]).then_inc(s_turn, 1)

                def body(i, first, last):
                    at = At(dve, i)
                    for g in range(IT):
                        conv(at, g, first)
                        if g == 0 and not first:
                            turn(at, IT - 1, 1, False)
                        elif g % 4 == 3 or g == 4:
                            turn(at, g - 1, 0, first)
                    if last:
                        turn(at, IT - 1, 0, False)

                run_bodies(dve, HALF, body)

            @block.gpsimd
            def _(pool):
                def body(i, first, last):
                    at = At(pool, i)
                    for u in range(2):
                        for m in range(2):
                            pool.wait_ge(s_turn, at(4, 2 * u + m + 1))
                            dst = v[u][:, bass.ds(i * (NC2 * HV // D), NC2 * HV // D), :].rearrange("p n (c d) -> p (n c) d", d=HV)
                            nc.gpsimd.tensor_copy(dst[:, :, m * 32:(m + 1) * 32], vt[:, m].rearrange("p (c i) -> p c i", i=C)).then_inc(s_v, 1)

                run_bodies(pool, HALF, body)


def unit_phase(nc, R, name, q, k, hblk):
    with phase(nc, name) as p:
        ones = p.sb("ones", [P, P])
        eps = p.sb("eps", [P, 2])
        sq = p.sb("sq", [P, 2, T])
        rt = p.sb("rt", [P, 2, T])
        ps = p.ps("ps", [P, 2, T])
        s_c, s_eps, s_sq, s_ss, s_rt, s_un = (p.sem(n) for n in ("c", "eps", "sq", "ss", "rt", "un"))
        with nc.Block() as block:
            @block.sync
            def _(sp):
                sp.dma_start(ones[:, :], hblk).then_inc(s_c, 16)

            @block.gpsimd
            def _(pool):
                nc.gpsimd.memset(eps[:, 0:1], HK * 1e-6)
                nc.gpsimd.memset(eps[:, 1:2], 1e-6).then_inc(s_eps, 1)

                def body(i, first, last):
                    at = At(pool, i)
                    for m in range(2):
                        if not first:
                            pool.wait_ge(s_ss, at(2, m - 1))
                        src = (q, k)[m][:, bass.ds(i * T, T)]
                        nc.gpsimd.tensor_tensor(sq[:, m], src, src, ALU.mult).then_inc(s_sq, 1)

                run_bodies(pool, B, body)

            @block.tensor
            def _(pe):
                pe.wait_ge(s_c, 16)

                def body(i, first, last):
                    at = At(pe, i)
                    for m in range(2):
                        pe.wait_ge(s_sq, at(2, m + 1))
                        if not first:
                            pe.wait_ge(s_rt, at(2, m - 1))
                        nc.tensor.matmul(ps[:, m], ones[:, :], sq[:, m], start=True, stop=True).then_inc(s_ss, 1)

                run_bodies(pe, B, body)

            @block.scalar
            def _(act):
                act.wait_ge(s_eps, 1)

                def body(i, first, last):
                    at = At(act, i)
                    for m in range(2):
                        act.wait_ge(s_ss, at(2, m + 1))
                        if not first:
                            act.wait_ge(s_un, at(2, m - 1))
                        nc.scalar.activation(rt[:, m], ps[:, m], ACT.Sqrt, bias=eps[:, m:m + 1], scale=1.0 if m else float(HK)).then_inc(s_rt, 1)

                run_bodies(act, B, body)

            @block.vector
            def _(dve):
                def body(i, first, last):
                    at = At(dve, i)
                    for m in range(2):
                        dst = (q, k)[m][:, bass.ds(i * T, T)]
                        dve.wait_ge(s_rt, at(2, m + 1))
                        nc.vector.reciprocal(rt[:, m], rt[:, m])
                        dve.drain()
                        dve.wait_ge(s_sq, at(2, m + 1))
                        nc.vector.tensor_tensor(dst, dst, rt[:, m], ALU.mult).then_inc(s_un, 1)

                run_bodies(dve, B, body)


def chunks_phase(nc, R, name, ab, q, k, kd, inv, at_, last_g, tiles):
    LV = (2, 4, 8, 16)
    with phase(nc, name) as p:
        cs = p.sb("cs", [P, 8, C])
        eye = p.sb("eye", [P, T])
        rep = p.sb("rep", [P, 2, 2, QT, P])
        brow = p.sb("brow", [P, 2, T])
        arow = p.sb("arow", [P, 2, T])
        a1 = p.sb("a1", [P, T])
        a0 = p.sb("a0", [P, T])
        M = p.sb("M", [P, 2, T])
        G = p.sb("G", [P, T])
        ks = p.sb("ks", [P, 2, T])
        qs = p.sb("qs", [P, 2, T])
        kt = p.sb("kt", [P, T])
        L = p.sb("L", [P, 2, T])
        Lm = p.sb("Lm", [P, 2, 2, T])
        X = p.sb("X", [P, 2, T])
        Xt = p.sb("Xt", [P, 2, T])
        Y = p.sb("Y", [P, 2, T])
        bc = p.sb("bc", [P, 2, T])
        pR = p.ps("pR", [P, 2, T])
        pK = p.ps("pK", [P, 2, T])
        pQ = p.ps("pQ", [P, 2, T])
        s_c, s_rep, s_row, s_rc, s_kq, s_T, s_Y, s_Yc, s_Z, s_end = (p.sem(n) for n in ("c", "rep", "row", "rc", "kq", "T", "Y", "Yc", "Z", "end"))
        c3 = lambda a: a.rearrange("p (c i) -> p c i", i=C)
        cst = lambda n: cs[:, n].rearrange("p (o i) -> p o i", o=1).broadcast_to([P, NC2, C])
        NL = len(LV)
        NBODY = B // 2

        def blocks(dst, lhs, rhs):
            for c in range(NC2):
                for h in range(H2):
                    rows, cols = slice(h * 32, h * 32 + 32), slice(c * C, (c + 1) * C)
                    ins = nc.tensor.matmul(dst[rows, cols], lhs[rows, cols], rhs[rows, cols], start=True, stop=True)
            return ins

        with nc.Block() as block:
            @block.sync
            def _(sp):
                sp.dma_start(cs[:, :, :], tiles).then_inc(s_c, 16)

            @block.tensor
            def _(pe):
                def body(i, first, last):
                    at = At(pe, i)
                    for u in range(2):
                        pe.wait_ge(s_rep, at(2, u + 1))
                        if not (first and u == 0):
                            pe.wait_ge(s_rc, at(2, u))
                        for m in range(2):
                            for j in range(QT):
                                ins = nc.tensor.transpose(pR[:, m, j * P:(j + 1) * P], rep[:, u, m, j], R.ident[:, :])
                        ins.then_inc(s_row, 1)
                    for u in range(2):
                        pe.wait_ge(s_rc, at(2, u + 1))
                        if not first:
                            pe.wait_ge(s_end, at(2, u - 1))
                        pe.nop(nofuse=True)
                        blocks(pK[:, u], ks[:, u], ks[:, u])
                        blocks(pQ[:, u], ks[:, u], qs[:, u]).then_inc(s_kq, 1)
                    for l in range(NL):
                        for u in range(2):
                            pe.wait_ge(s_T, at(2 * NL, 2 * l + u + 1))
                            pe.nop(nofuse=True)
                            blocks(pK[:, u], Lm[:, u, l % 2], X[:, u]).then_inc(s_Y, 1)
                        for u in range(2):
                            pe.wait_ge(s_Yc, at(2 * NL, 2 * l + u + 1))
                            pe.nop(nofuse=True)
                            blocks(pQ[:, u], Y[:, u], Xt[:, u]).then_inc(s_Z, 1)

                run_bodies(pe, NBODY, body)

            @block.scalar
            def _(act):
                def body(i, first, last):
                    at = At(act, i)
                    for u in range(2):
                        act.wait_ge(s_row, at(2, u + 1))
                        if not first:
                            act.wait_ge(s_end, at(2, u - 1))
                        nc.scalar.activation(brow[:, u], pR[:, 0], ACT.Copy)
                        nc.scalar.activation(arow[:, u], pR[:, 1], ACT.Copy)
                        nc.scalar.activation(qs[:, u], q[:, bass.ds((i * 2 + u) * T, T)], ACT.Copy)
                        nc.scalar.activation(ks[:, u], k[:, bass.ds((i * 2 + u) * T, T)], ACT.Copy).then_inc(s_rc, 1)
                    for l in range(NL):
                        for u in range(2):
                            act.wait_ge(s_Y, at(2 * NL, 2 * l + u + 1))
                            if l == 0 and not first:
                                act.wait_ge(s_Z, at(2 * NL, u - 1))
                            nc.scalar.activation(Y[:, u], pK[:, u], ACT.Copy).then_inc(s_Yc, 1)

                run_bodies(act, NBODY, body)

            @block.vector
            def _(dve):
                V = nc.vector

                def then(ins):
                    dve.drain()

                dve.wait_ge(s_c, 16)
                then(V.tensor_copy(c3(eye[:, :]), cst(5)))

                def repeat(at, i, u, first):
                    if not first:
                        dve.wait_ge(s_row, at(2, u - 1))
                    src = ab[:, bass.ds((i * 2 + u) * QT, QT), :, :]
                    for m in range(2):
                        for h in range(H2):
                            ins = V.tensor_copy(rep[:, u, m, :, h * 32:(h + 1) * 32], src[:, :, m, h:h + 1].broadcast_to([P, QT, 32]))
                    ins.then_inc(s_rep, 1)

                def prepare(at, i, u):
                    cols = bass.ds((i * 2 + u) * T, T)
                    dve.drain()
                    dve.wait_ge(s_rc, at(2, u + 1))
                    V.tensor_tensor(c3(a1[:, :]), c3(arow[:, u]), cst(7), ALU.mult)
                    then(V.tensor_tensor(c3(a0[:, :]), c3(arow[:, u]), cst(6), ALU.mult))
                    V.tensor_tensor_scan(M[:, u], a1[:, :], eye[:, :], 0.0, ALU.mult, ALU.add)
                    V.tensor_tensor_scan(G[:, :], a1[:, :], a0[:, :], 0.0, ALU.mult, ALU.add)
                    V.transpose(kt[:, :], ks[:, u])
                    then(V.transpose(bc[:, u], brow[:, u]))
                    V.tensor_copy(last_g[:, bass.ds(i * 2 + u, 1), :].rearrange("p o c -> p (o c)"), c3(G[:, :])[:, :, C - 1])
                    V.tensor_tensor(c3(kd[:, cols]), c3(kt[:, :]), c3(M[:, u])[:, :, C - 1:].broadcast_to([P, NC2, C]), ALU.mult)
                    dve.wait_ge(s_kq, at(2, u + 1))
                    V.tensor_tensor(L[:, u], pK[:, u], M[:, u], ALU.mult)
                    V.tensor_tensor(at_[:, cols], pQ[:, u], M[:, u], ALU.mult)
                    dve.drain()
                    then(V.tensor_tensor(L[:, u], L[:, u], brow[:, u], ALU.mult))
                    V.tensor_tensor(c3(Lm[:, u, 0]), c3(L[:, u]), cst(1), ALU.mult)
                    then(V.tensor_tensor(c3(Xt[:, u]), c3(L[:, u]), cst(0), ALU.mult))
                    then(V.tensor_tensor(Xt[:, u], Xt[:, u], eye[:, :], ALU.add))
                    V.transpose(X[:, u], Xt[:, u]).then_inc(s_T, 1)
                    V.tensor_tensor(q[:, cols], q[:, cols], G[:, :], ALU.mult)
                    V.tensor_tensor(k[:, cols], k[:, cols], G[:, :], ALU.mult)

                def join(at, i, l, u):
                    cols = bass.ds((i * 2 + u) * T, T)
                    if l + 1 < NL:
                        V.tensor_tensor(c3(Lm[:, u, (l + 1) % 2]), c3(L[:, u]), cst(l + 2), ALU.mult)
                    dve.drain()
                    dve.wait_ge(s_Z, at(2 * NL, 2 * l + u + 1))
                    V.tensor_tensor(Xt[:, u], pQ[:, u], Xt[:, u], ALU.add)
                    dve.drain()
                    if l + 1 < NL:
                        V.transpose(X[:, u], Xt[:, u]).then_inc(s_T, 1)
                    else:
                        V.tensor_tensor(inv[:, cols], Xt[:, u], bc[:, u], ALU.mult).then_inc(s_end, 1)

                def body(i, first, last):
                    at = At(dve, i)
                    for u in range(2):
                        repeat(at, i, u, first)
                    for u in range(2):
                        prepare(at, i, u)
                    for l in range(NL):
                        for u in range(2):
                            join(at, i, l, u)

                run_bodies(dve, NBODY, body)


def recur_phase(nc, R, name, q, k, kd, inv, at_, last_g, v):
    with phase(nc, name) as p:
        GW = HALF * HV
        st = p.sb("st", [P, 4, 5, HALF, C])
        S = p.sb("S", [P, 2, 2, HALF, HV])
        Sg = p.sb("Sg", [P, 2, HALF, HV])
        Rr = p.sb("Rr", [P, 2, HALF, HV])
        U = p.sb("U", [P, 2, HALF, HV])
        pA = p.ps("pA", [P, 2, T])
        pU = p.ps("pU", [P, 2, T])
        pS = p.ps("pS", [P, 2, T])
        pO = p.ps("pO", [P, 2, T])
        s_z = p.sem("z")
        s_st = p.sem("st")
        s_st2 = p.sem("st2")
        s_A, s_R, s_U, s_Uc, s_Sd, s_S, s_O, s_Oc = (p.sem(n) for n in ("A", "R", "U", "Uc", "Sd", "S", "O", "Oc"))
        IT = 4
        NBODY = NC2 // 2
        seqs = lambda a, g, c: a[:, g * HALF * T:(g + 1) * HALF * T].rearrange("p (b c i) -> p b c i", b=HALF, i=C)[:, :, bass.ds(c, 1), :].rearrange("p b o i -> p b (o i)")
        w4 = lambda a: a[:, :GW].rearrange("p (b d) -> p b d", d=HV)

        def vchunk(g, c):
            return v[g][:, :, :].rearrange("p (b n) (c d) -> p b (n c) d", b=HALF, d=HV)[:, :, bass.ds(c, 1), :].rearrange("p b o d -> p b (o d)")

        with nc.Block() as block:
            @block.gpsimd
            def _(pool):
                def body(i, first, last):
                    at = At(pool, i)
                    for n in range(IT):
                        cc, g = divmod(n, 2)
                        if not first:
                            pool.wait_ge(s_O, at(IT, n - 3))
                        for m, src in enumerate((k, q, kd)):
                            ins = nc.gpsimd.tensor_copy(st[:, n, m], seqs(src, g, i * 2 + cc))
                        ins.then_inc(s_st, 1)

                run_bodies(pool, NBODY, body)

            @block.tensor
            def _(pe):
                def small(dst, lhs, rhs):
                    pe.nop(nofuse=True)
                    for b in range(HALF):
                        for h in range(H2):
                            r = slice(h * 32, h * 32 + 32)
                            ins = nc.tensor.matmul(dst[r, b], lhs[r, b], rhs[r, b], start=True, stop=True)
                    return ins

                def body(i, first, last):
                    at = At(pe, i)
                    if first:
                        pe.wait_ge(s_z, 1)
                    for cc in range(2):
                        begin = first and cc == 0
                        for g in range(2):
                            n = cc * 2 + g
                            pe.wait_ge(s_st, at(IT, n + 1))
                            if not begin:
                                pe.wait_ge(s_S, at(IT, n - 1))
                            small(w4(pA[:, g]), st[:, n, 0], S[:, g, cc]).then_inc(s_A, 1)
                        for g in range(2):
                            n = cc * 2 + g
                            pe.wait_ge(s_st2, at(IT, n + 1))
                            pe.wait_ge(s_R, at(IT, n + 1))
                            small(w4(pU[:, g]), st[:, n, 3], Rr[:, g]).then_inc(s_U, 1)
                        for g in range(2):
                            n = cc * 2 + g
                            pe.wait_ge(s_Uc, at(IT, n + 1))
                            small(w4(pS[:, g]), st[:, n, 2], U[:, g]).then_inc(s_Sd, 1)
                        for g in range(2):
                            n = cc * 2 + g
                            if not begin:
                                pe.wait_ge(s_Oc, at(IT, n - 1))
                            pe.nop(nofuse=True)
                            for b in range(HALF):
                                for h in range(H2):
                                    r = slice(h * 32, h * 32 + 32)
                                    nc.tensor.matmul(w4(pO[:, g])[r, b], st[r, n, 1, b], S[r, g, cc, b], start=True, stop=False)
                                    ins = nc.tensor.matmul(w4(pO[:, g])[r, b], st[r, n, 4, b], U[r, g, b], start=False, stop=True)
                            ins.then_inc(s_O, 1)

                run_bodies(pe, NBODY, body)

            @block.scalar
            def _(act):
                def fix(at, i, n, first, ahead):
                    cc, g = divmod(n % IT, 2)
                    if not (first and n < IT):
                        act.wait_ge(s_O, at(IT, n - 3))
                    for m, src in ((3, inv), (4, at_)):
                        ins = nc.scalar.activation(st[:, n % IT, m], seqs(src, g, i * 2 + cc + (n // IT) * 2), ACT.Copy)
                    ins.then_inc(s_st2, 1)

                def body(i, first, last):
                    at = At(act, i)
                    if first:
                        fix(at, i, 0, True, 0)
                        fix(at, i, 1, True, 0)
                    for cc in range(2):
                        for g in range(2):
                            n = cc * 2 + g
                            act.wait_ge(s_U, at(IT, n + 1))
                            if not (first and cc == 0):
                                act.wait_ge(s_O, at(IT, n - 1))
                            nc.scalar.activation(U[:, g], w4(pU[:, g]), ACT.Copy).then_inc(s_Uc, 1)
                        for g in range(2):
                            n = cc * 2 + g
                            if not (last and n + 2 >= IT):
                                fix(at, i, n + 2, first, 0)
                        for g in range(2):
                            n = cc * 2 + g
                            act.wait_ge(s_O, at(IT, n + 1))
                            nc.scalar.activation(vchunk(g, i * 2 + cc), w4(pO[:, g]), ACT.Copy).then_inc(s_Oc, 1)

                run_bodies(act, NBODY, body)

            @block.vector
            def _(dve):
                nc.vector.memset(S[:, :, :, :, :], 0.0).then_inc(s_z, 1)
                dve.drain()

                def body(i, first, last):
                    at = At(dve, i)
                    for cc in range(2):
                        begin = first and cc == 0
                        for g in range(2):
                            n = cc * 2 + g
                            dve.wait_ge(s_A, at(IT, n + 1))
                            if not begin:
                                dve.wait_ge(s_U, at(IT, n - 1))
                            nc.vector.scalar_tensor_tensor(out=Rr[:, g], in0=w4(pA[:, g]), scalar=-1.0, in1=vchunk(g, i * 2 + cc),
                                                           op0=ALU.mult, op1=ALU.add).then_inc(s_R, 1)
                            gl = last_g[:, g * HALF:(g + 1) * HALF, bass.ds(i * 2 + cc, 1)].broadcast_to([P, HALF, HV])
                            nc.vector.tensor_tensor(Sg[:, g], S[:, g, cc], gl, ALU.mult)
                        dve.drain()
                        for g in range(2):
                            n = cc * 2 + g
                            dve.wait_ge(s_Sd, at(IT, n + 1))
                            if not begin:
                                dve.wait_ge(s_O, at(IT, n - 1))
                            nc.vector.tensor_tensor(S[:, g, 1 - cc], w4(pS[:, g]), Sg[:, g], ALU.add).then_inc(s_S, 1)
                        dve.drain()

                run_bodies(dve, NBODY, body)


def output2_phase(nc, R, name, o, wg, nw, wo, xn, y_all):
    with phase(nc, name) as p:
        wgs = p.sb("wgs", [P, 2, P])
        wos = p.sb("wos", [P, 2, D])
        nws = p.sb("nws", [P, 2])
        eps = p.sb("eps", [P, 1])
        sq = p.sb("sq", [P, 2, NC2 * HV])
        ss = p.sb("ss", [P, 2, NC2])
        on = p.sb("on", [P, 2, 2, T])
        ot = p.sb("ot", [P, 2, T])
        sg = p.sb("sg", [P, 2, 2, T])
        gt = p.sb("gt", [P, 2, 2, T])
        xr = p.sb("xr", [P, 2, QT, D])
        pg = p.ps("pg", [P, 4, T])
        py = p.ps("py", [P, 2, T])
        s_w, s_eps, s_g, s_sg, s_ss, s_rt, s_gt, s_y, s_o = (p.sem(n) for n in ("w", "eps", "g", "sg", "ss", "rt", "gt", "y", "o"))
        s_x = [p.sem("x0"), p.sem("x1")]
        with nc.Block() as block:
            @block.sync
            def _(sp):
                for dst, src in ((wgs[:, :, :], wg), (wos[:, :, :], wo), (nws[:, :], nw)):
                    sp.dma_start(dst, src).then_inc(s_w, 16)

                def body(i, first, last):
                    at = At(sp, i)
                    for u in range(2):
                        if not first:
                            sp.wait_ge(s_o, at(2, u - 1))
                        src = xn[:, bass.ds((i + u * HALF) * QT, QT), :]
                        sp.dma_start(xr[:, u], src).then_inc(s_x[u], 16)

                run_bodies(sp, HALF, body)

            @block.tensor
            def _(pe):
                pe.wait_ge(s_w, 48)

                def gates(at, i, u, first, back=0):
                    if not first:
                        pe.wait_ge(s_sg, at(2, u - 1))
                    for m in range(2):
                        ins = nc.tensor.matmul(pg[:, u * 2 + m], wgs[:, m], R.xn2T[:, bass.ds((i + u * HALF) * T, T)], start=True, stop=True)
                    ins.then_inc(s_g, 1)

                def body(i, first, last):
                    at = At(pe, i)
                    for u in range(2):
                        gates(at, i, u, first)
                    for u in range(2):
                        pe.wait_ge(s_gt, at(2, u + 1))
                        if not first:
                            pe.wait_ge(s_o, at(2, u - 1))
                        for j in range(QT):
                            for m in range(2):
                                ins = nc.tensor.matmul(py[:, u, j * P:(j + 1) * P], gt[:, u, m, j * P:(j + 1) * P], wos[:, m], start=(m == 0), stop=(m == 1))
                        ins.then_inc(s_y, 1)

                run_bodies(pe, HALF, body)

            @block.scalar
            def _(act):
                act.wait_ge(s_eps, 1)

                def body(i, first, last):
                    at = At(act, i)
                    for u in range(2):
                        act.wait_ge(s_g, at(2, u + 1))
                        if not first:
                            act.wait_ge(s_gt, at(2, u - 1))
                        nc.scalar.activation(sg[:, u], pg[:, u * 2:u * 2 + 2], ACT.Silu).then_inc(s_sg, 1)
                    for u in range(2):
                        act.wait_ge(s_ss, at(2, u + 1))
                        nc.scalar.activation(ss[:, u], ss[:, u], ACT.Sqrt, bias=eps[:, :], scale=1.0 / HV).then_inc(s_rt, 1)

                run_bodies(act, HALF, body)

            @block.vector
            def _(dve):
                V = nc.vector
                V.memset(eps[:, :], EPS).then_inc(s_eps, 1)
                dve.wait_ge(s_w, 48)
                src = lambda i, u: o[u][:, bass.ds(i * NC2 * HV // D, NC2 * HV // D), :].rearrange("p n (c d) -> p (n c) d", d=HV)

                def body(i, first, last):
                    at = At(dve, i)
                    for u in range(2):
                        s3 = sq[:, u].rearrange("p (c d) -> p c d", d=HV)
                        V.tensor_tensor(s3, src(i, u), src(i, u), ALU.mult)
                        dve.drain()
                        V.reduce_sum(ss[:, u], s3, AX.X).then_inc(s_ss, 1)
                    for u in range(2):
                        dve.wait_ge(s_rt, at(2, u + 1))
                        V.reciprocal(ss[:, u], ss[:, u])
                        dve.drain()
                        for m in range(2):
                            V.tensor_tensor(on[:, u, m].rearrange("p (c d) -> p c d", d=32), src(i, u)[:, :, m * 32:(m + 1) * 32],
                                            ss[:, u].rearrange("p (c o) -> p c o", o=1).broadcast_to([P, NC2, 32]), ALU.mult)
                        dve.drain()
                        for m in range(2):
                            V.transpose(ot[:, m], on[:, u, m])
                        dve.drain()
                        dve.wait_ge(s_sg, at(2, u + 1))
                        if not first:
                            dve.wait_ge(s_y, at(2, u - 1))
                        for m in range(2):
                            ins = V.scalar_tensor_tensor(out=gt[:, u, m], in0=ot[:, m], scalar=nws[:, m:m + 1], in1=sg[:, u, m], op0=ALU.mult, op1=ALU.mult)
                        ins.then_inc(s_gt, 1)
                        dve.drain()
                    for u in range(2):
                        dve.wait_ge(s_y, at(2, u + 1))
                        dve.wait_ge(s_x[u], at(16, 16))
                        V.tensor_tensor(y_all[:, bass.ds((i + u * HALF) * T, T)], py[:, u], xr[:, u].rearrange("p q d -> p (q d)"), ALU.add).then_inc(s_o, 1)

                run_bodies(dve, HALF, body)


def layer2_attention(nc, R, t):
    with ExitStack() as ctx:
        keep = lambda name, shape: ctx.enter_context(nc.sbuf_tensor(name, shape, F32))
        park = {n: nc.dram_tensor(f"park_{n}", (P, NT, D), F32).ap() for n in "xsf"}
        lg = keep("lg2a", [P, NT, 2 * H2])
        ab = keep("ab", [P, NT, 2, H2])
        last_g = keep("last_g", [P, B, NC2])
        kd, inv, at_ = keep("kd", [P, B * T]), keep("inv", [P, B * T]), keep("at", [P, B * T])
        with phase(nc, "park") as p:
            s_out = p.sem("out")
            with nc.Block() as block:
                @block.sync
                def _(sp):
                    for n in "xsf":
                        sp.dma_start(park[n], {"x": R.x, "s": R.s, "f": R.f}[n][:, :, :]).then_inc(s_out, 16)
            logits_phase(nc, R, "lg_2a", t["wba"], t["bba"], 2 * H2, lg, xT=R.xn2T)
            decay_phase(nc, R, "decay", lg, ab, t["alog"])
            with nc.Block() as block:
                @block.sync
                def _(sp):
                    sp.wait_ge(s_out, 48)
        q = R.xnT[:, :]
        k = R.f[:, :, :].rearrange("p n d -> p (n d)")
        v = (R.x, R.s)
        conv_phase(nc, R, "conv", t["w2a"], t["taps"], q, k, v)
        unit_phase(nc, R, "unit", q, k, t["hblk"])
        chunks_phase(nc, R, "chunks", ab, q, k, kd, inv, at_, last_g, t["tiles2"])
        recur_phase(nc, R, "recur", q, k, kd, inv, at_, last_g, v)
        output2_phase(nc, R, "out2", v, t["wg2"], t["nw2"], t["wo2"], park["s"], q)
        with phase(nc, "unpark") as p:
            s_in = p.sem("in")
            with nc.Block() as block:
                @block.sync
                def _(sp):
                    for n in "xf":
                        sp.dma_start({"x": R.x, "f": R.f}[n][:, :, :], park[n]).then_inc(s_in, 16)
                    sp.wait_ge(s_in, 32)

                @block.vector
                def _(dve):
                    nc.vector.tensor_copy(R.s[:, :, :].rearrange("p n d -> p (n d)"), q)


def layer0(nc, R, t, before):
    norm_phase(nc, R, "norm0", before)
    layer0_attention(nc, R, t)
    layer0_gate(nc, R, t)


def layer1(nc, R, t, before):
    norm_phase(nc, R, "norm1", before)
    layer1_attention(nc, R, t)
    layer1_gate(nc, R, t)


def layer2(nc, R, t, before):
    with ExitStack() as ctx:
        R.xn2T = ctx.enter_context(nc.sbuf_tensor("xn2T", [P, B * T], F32))
        wb = ctx.enter_context(nc.sbuf_tensor("ln2", [P, 2], F32))
        with phase(nc, "ln2w") as p:
            s_w = p.sem("w")
            with nc.Block() as block:
                @block.sync
                def _(sp):
                    sp.dma_start(wb[:, :], t["ln2"]).then_inc(s_w, 16)
                    sp.wait_ge(s_w, 16)
        norm_phase(nc, R, "norm2", before, second=(wb[:, 0:1], wb[:, 1:2]), store=R.s)
        layer2_gate(nc, R, t)
        layer2_attention(nc, R, t)


def layer3(nc, R, t, before):
    norm_phase(nc, R, "norm3", before)
    layer3_attention(nc, R, t)
    layer3_gate(nc, R, t)


LAYERS = {0: layer0, 1: layer1, 2: layer2, 3: layer3}


def layout(inp):
    f = lambda a: np.ascontiguousarray(a)
    rows = lambda a, *shape: f(np.broadcast_to(a, (P, *shape)))
    t = {"x": f(inp["L0_attn_inputs"]), "ident": np.eye(P, dtype=np.float32)}
    for k in ("wq0", "wk0", "wq1", "wk1", "wv", "wo"):
        t[k] = f(inp[f"L0_attn_{k}"])
    for k in range(4):
        t[f"l{k}"] = f(inp[f"L0_attn_l{k}"])
    t["zero4"] = np.zeros((P, 4), np.float32)
    t["zero1"] = np.zeros((P, 1), np.float32)
    q, c = np.arange(P)[:, None], np.arange(T + (QT - 1) * P)[None, :]
    dist = (c - (QT - 1) * P) - q
    slopes = 2.0 ** (-8.0 * np.arange(1, NH + 1) / NH)
    t["gain0"] = np.tile(slopes, (P, B)).astype(np.float32)
    pos, one = np.arange(T), np.ones(T)
    hi, lo8 = pos // 256 * 256, pos % 256
    t["ext0"] = f(np.stack([[one, one, -hi, -lo8] + [0 * one] * 3, [hi, lo8, one, one] + [one] * 3]).transpose(1, 0, 2).astype(np.float32))
    t["ext1"] = f(np.stack([np.zeros((3, T)), np.ones((3, T))]).transpose(1, 0, 2).astype(np.float32))
    later = np.where(np.arange(P)[None] > np.arange(P)[:, None], np.float32(-1e30), np.float32(0))
    t["masks"] = f(np.stack([later, later.T, np.eye(P, dtype=np.float32)], 1))
    t["qscale0"] = np.repeat(DH ** -0.5 / slopes, DH)[:, None].astype(np.float32)
    t["ln_w0"] = rows(inp["L0_attn_ln_w"].reshape(1, NH * DH), QT, NH * DH)
    t["ln_b0"] = rows(inp["L0_attn_ln_b"].reshape(1, NH * DH), QT, NH * DH)
    def experts(w1, b1, w2):
        e, _, ff = w1.shape
        u = ff // P
        return (f(w1), f(b1.reshape(e, u, P).transpose(2, 0, 1)), f(w2.reshape(e, u, P, D).transpose(0, 2, 1, 3).reshape(e, P, u * D)))

    t["gw0"], t["gb0"] = f(inp["L0_ffn_gate_w"]), f(inp["L0_ffn_gate_b"][:, None])
    t["w1_0"], t["b1_0"], t["w2_0"] = experts(*(np.concatenate([inp[f"L0_ffn_r{k}"], inp[f"L0_ffn_s{k}"]]) for k in ("w1", "b1", "w2")))
    t["b2_0"] = np.concatenate([inp["L0_ffn_rb2"], inp["L0_ffn_sb2"]])
    for n in (4, 8):
        t[f"lower{n}"] = rows(np.tril(np.ones((n, n)), -1).reshape(1, n * n).astype(np.float32), n * n)
    t["Wq1"], t["Wk1"], t["Wv1"], t["Wo1"] = (f(inp[f"L1_attn_W{k}"]) for k in "qkvo")
    t["bqk1"] = f(np.stack([inp["L1_attn_bq"], inp["L1_attn_bk"]], 1))
    t["bv1"] = f(inp["L1_attn_bv"][:, None])
    t["bo1"] = rows(inp["L1_attn_bo"][None], QT, D)
    t["hmask"] = np.repeat(np.eye(NH, dtype=np.float32), DH, 0)
    t["gain1"] = np.full((P, B * NH), DH ** -0.5, np.float32)
    t["rw1"], t["rb1"] = f(inp["L1_ffn_router_w"].T), np.zeros((64, 1), np.float32)
    t["cbias"] = rows(inp["L1_ffn_correction_bias"][None], 64)
    up = inp["L1_ffn_up_w"].reshape(32, 2, P, 64).transpose(0, 2, 1, 3).reshape(32, P, P)
    t["up1"] = np.concatenate([up, inp["L1_ffn_shared_up_w"].reshape(P, 2, P).transpose(1, 0, 2)])
    t["down1"] = np.concatenate([inp["L1_ffn_down_w"].reshape(32, P, D), inp["L1_ffn_shared_down_w"].reshape(2, P, D)])
    sel = np.zeros((34, P, 2, 2, 64), np.float32)
    for e in range(64):
        sel[e // 2, e, :, e % 2] = 1
        sel[e // 2, 64 + e, 0, e % 2] = 1
    sel[32:, 64, 1] = 1
    t["sel1"] = sel.reshape(34, P, 2 * P)
    t["gw2"], t["gb2"] = f(inp["L2_ffn_gate_w"]), f(inp["L2_ffn_gate_b"][:, None])
    t["w1_2"], t["b1_2"], t["w2_2"] = experts(*(inp[f"L2_ffn_{k}"] for k in ("w1", "b1", "w2")))
    t["b2_2"] = f(inp["L2_ffn_b2"])
    t["upto"] = np.triu(np.ones((P, P), np.float32))
    t["ones"] = np.ones((P, P), np.float32)
    g, u, dn = (inp[f"L3_ffn_w_{k}"] for k in ("gate", "up", "down"))
    t["w3"] = f(np.stack([g.T.reshape(P, 3, P), u.T.reshape(P, 3, P), dn.T.reshape(3, P, P).transpose(1, 0, 2)], 1).reshape(P, 9 * P))
    t["w3a"] = f(np.stack([inp[f"L3_attn_W{k}"].reshape(P, 8, P).transpose(1, 0, 2) for k in "qkv"], 2).reshape(8, P, 3 * P))
    t["wo3"] = f(inp["L3_attn_Wo"].reshape(8, P, D))
    t["bo3"] = rows(np.tile(inp["L3_attn_bo"], QT)[None], QT * D)
    b3 = inp["L3_attn_rel_pos_bias"][:, np.clip(P - 1 + dist, 0, P - 1)]
    b3 = np.where(dist > 0, np.float32(-1e30), b3)
    t["bias3"] = f(b3.transpose(1, 0, 2).reshape(P, 8, -1))
    t["wba"] = f(np.concatenate([inp["L2_attn_Wb"], inp["L2_attn_Wa"]], 1))
    t["bba"] = np.concatenate([np.zeros(H2, np.float32), inp["L2_attn_dt_bias"]])[:, None]
    t["alog"] = rows(inp["L2_attn_A_log"][None], H2)
    t["ln2"] = f(np.stack([inp["L2_attn_ln_w"], inp["L2_attn_ln_b"]], 1))
    order = np.arange(H2 * HV).reshape(H2, 2, 32).transpose(1, 0, 2)
    blocks = lambda w: w[:, order.reshape(-1)].reshape(-1, 2, P)
    t["w2a"] = f(np.concatenate([inp["L2_attn_Wq"][:, None], inp["L2_attn_Wk"][:, None], blocks(inp["L2_attn_Wv"])], 1))
    t["taps"] = f(np.concatenate([inp["L2_attn_conv_q"][None], inp["L2_attn_conv_k"][None], inp["L2_attn_conv_v"][order.reshape(2, P)]]).transpose(1, 0, 2))
    t["hblk"] = np.kron(np.eye(H2, dtype=np.float32), np.ones((32, 32), np.float32))
    t["wg2"] = f(blocks(inp["L2_attn_Wg"]))
    t["nw2"] = f(np.tile(inp["L2_attn_norm_w"].reshape(2, 1, 32), (1, H2, 1)).reshape(2, P).T)
    t["wo2"] = f(inp["L2_attn_Wo"][order.reshape(2, P)].transpose(1, 0, 2))
    j, i = np.arange(C)[:, None], np.arange(C)[None, :]
    masks = [np.where((i // (2 * s) == j // (2 * s)) & (i // s > j // s), -1.0, 0.0) for s in (1, 2, 4, 8, 16)]
    consts = masks + [np.eye(C), np.broadcast_to(i == 0, (C, C)), np.broadcast_to(i > 0, (C, C))]
    t["tiles2"] = f(np.tile(np.stack(consts, 1).astype(np.float32), (H2, 1, 1)))
    return t


class Resident:
    pass


def program(nc, t, out, layers=(0, 1, 2, 3), dbg=None):
    with ExitStack() as ctx:
        R = Resident()

        def keep(name, shape, dt=F32):
            return ctx.enter_context(nc.sbuf_tensor(name, shape, dt))

        R.x = keep("x", [P, NT, D])
        R.xnT = keep("xnT", [P, B * T])
        R.s = keep("s", [P, NT, D])
        R.f = keep("f", [P, NT, D])
        R.ident = keep("ident", [P, P])
        load_phase(nc, R, t)
        for n, layer in enumerate(layers):
            before = n > 0
            LAYERS[layer](nc, R, t, before)
        final_phase(nc, R, out)


def load_phase(nc, R, t):
    with phase(nc, "load") as p:
        s_in = p.sem("in")
        with nc.Block() as block:
            @block.sync
            def _(sp):
                xs = t["x"].rearrange("b (q p) d -> p (b q) d", p=P)
                for h in range(4):
                    sp.dma_start(R.x[:, h * 8:(h + 1) * 8, :], xs[:, h * 8:(h + 1) * 8, :]).then_inc(s_in, 16)
                sp.dma_start(R.ident[:, :], t["ident"]).then_inc(s_in, 16)
                sp.wait_ge(s_in, 80)


def final_phase(nc, R, out):
    with phase(nc, "final") as p:
        ex = p.sb("ex", [P, 2, T])
        s_exp, s_dve, s_y, s_out = p.sem("exp"), p.sem("dve"), p.sem("y"), p.sem("out")
        od = out.rearrange("b (q p) d -> p (b q) d", p=P)
        with nc.Block() as block:
            @block.scalar
            def _(act):
                for n in range(B):
                    if n >= 2:
                        act.wait_ge(s_dve, 2 * (n - 1))
                    nc.scalar.activation(ex[:, n % 2], R.f[:, n * QT:(n + 1) * QT, :].rearrange("p a d -> p (a d)"),
                                         ACT.Silu).then_inc(s_exp, 1)

            @block.vector
            def _(dve):
                c = Chain(dve, s_dve, 2)
                for n in range(B):
                    c.step(n)
                    e = ex[:, n % 2]
                    s, x = (a[:, n * QT:(n + 1) * QT, :].rearrange("p a d -> p (a d)") for a in (R.s, R.x))
                    dve.wait_ge(s_exp, n + 1)
                    c.link(nc.vector.tensor_tensor(e, e, s, ALU.mult))
                    c.did(nc.vector.tensor_tensor(x, e, x, ALU.add))

            @block.sync
            def _(sp):
                for n in range(B):
                    sp.wait_ge(s_dve, 2 * (n + 1))
                    sp.dma_start(od[:, n * QT:(n + 1) * QT, :], R.x[:, n * QT:(n + 1) * QT, :]).then_inc(s_out, 16)
                sp.wait_ge(s_out, 16 * B)


def kernel(**inputs):
    import numpy as _np
    import concourse.bacc as _bacc
    from concourse import mybir as _mybir
    from concourse.bass_utils import run_bass_kernel_spmd as _run

    nc = _bacc.Bacc("TRN2", target_bir_lowering=False, num_devices=1)
    arrays, t = {}, {}
    for name, a in layout({k: _np.asarray(v) for k, v in inputs.items()}).items():
        a = _np.ascontiguousarray(a)
        arrays[f"in_{name}_dram"] = a
        t[name] = nc.dram_tensor(f"in_{name}_dram", a.shape, _mybir.dt.from_np(a.dtype), kind="ExternalInput").ap()
    out = nc.dram_tensor("out_0_dram", (B, T, D), F32, kind="ExternalOutput").ap()
    program(nc, t, out)
    r = _run(nc, [arrays], core_ids=[0])
    return r.results[0]["out_0_dram"]
```
